# Optimizing a Trainium2 kernel written in Bass

```python
import numpy as np
import jax
import jax.numpy as jnp

def _softmax(x, axis=-1):
    return jax.nn.softmax(x, axis=axis)
def _gelu(x):
    return jax.nn.gelu(x, approximate=True)
def _silu(x):
    return jax.nn.silu(x)
def _sigmoid(x):
    return jax.nn.sigmoid(x)
def _layernorm(x, axis=-1, eps=1e-5):
    m = jnp.mean(x, axis=axis, keepdims=True)
    v = jnp.var(x, axis=axis, keepdims=True)
    return (x - m) / jnp.sqrt(v + eps)
def _scatter_add(tgt, idx, src, axis=0):
    return tgt.at[idx].add(src)
def _segment_sum(src, seg, n):
    return jax.ops.segment_sum(src, seg, n)

kernel_name = 'mk_conv_preact_d2_conv_nchw8_9cf242'

def setup_inputs(seed: int = 0):
    np.random.seed(seed)
    _w = jnp.asarray
    def _rec_inputs():
        import jax
        import jax.numpy as jnp
        _gk = jax.random.key(seed)
        x = -0.0001546 + 1 * jax.random.normal(jax.random.fold_in(_gk, 1), (8, 8, 1024, 1024), jnp.float32)
        return x
    x = _rec_inputs()
    def _L0_conv_setup():
        import jax, jax.numpy as jnp
        import numpy as np
        key = jax.random.key(seed)
        k1, k2, k3 = jax.random.split(key, 3)
        x = jax.random.normal(k1, (16, 8, 1024, 1024), dtype=jnp.float32)
        weight = jax.random.normal(k2, (8, 8, 3, 3), dtype=jnp.float32) * 0.1
        bias = jax.random.normal(k3, (8,), dtype=jnp.float32) * 0.1
        return {'x': x, 'weight': weight, 'bias': bias}
    _L0_conv_all = _L0_conv_setup()
    _L0_conv_in = {k: v for k, v in _L0_conv_all.items() if k in ('weight', 'bias', )}
    del _L0_conv_all

    def _L1_conv_setup():
        import jax, jax.numpy as jnp
        import numpy as np
        import math
        B, C_IN, C_OUT = (32, 8, 8)
        H, W = (1024, 1024)
        KH, KW = (3, 3)
        STRIDE = 1
        PAD = 1
        key = jax.random.key(seed)
        k1, k2, k3 = jax.random.split(key, 3)
        stdv = math.sqrt(1.0 / (C_IN * KH * KW))
        x = jax.random.normal(k1, (B, C_IN, H, W), dtype=jnp.float32)
        weight = jax.random.uniform(k2, (C_OUT, C_IN, KH, KW), dtype=jnp.float32, minval=-stdv, maxval=stdv)
        bias = jax.random.uniform(k3, (C_OUT,), dtype=jnp.float32, minval=-stdv, maxval=stdv)
        return {'input': x, 'weight': weight, 'bias': bias}
    _L1_conv_all = _L1_conv_setup()
    _L1_conv_in = {k: v for k, v in _L1_conv_all.items() if k in ('weight', 'bias', )}
    del _L1_conv_all

    return {
        "x": x,
        "L0_conv_weight": _L0_conv_in["weight"],
        "L0_conv_bias": _L0_conv_in["bias"],
        "L1_conv_weight": _L1_conv_in["weight"],
        "L1_conv_bias": _L1_conv_in["bias"],
    }

def reference(x, L0_conv_weight, L0_conv_bias, L1_conv_weight, L1_conv_bias):
    import jax
    import jax.numpy as jnp
    def _L0_conv_ref(x, weight, bias):
        import jax, jax.numpy as jnp
        import numpy as np
        out = jax.lax.conv_general_dilated(x, weight, window_strides=(1, 1), padding=((1, 1), (1, 1)), dimension_numbers=('NCHW', 'OIHW', 'NCHW'))
        return out + bias[None, :, None, None]

    def _L1_conv_ref(input, weight, bias):
        import jax, jax.numpy as jnp
        import numpy as np
        import math
        B, C_IN, C_OUT = (32, 8, 8)
        H, W = (1024, 1024)
        KH, KW = (3, 3)
        STRIDE = 1
        PAD = 1
        out = jax.lax.conv_general_dilated(input, weight, window_strides=(STRIDE, STRIDE), padding=[(PAD, PAD), (PAD, PAD)], dimension_numbers=('NCHW', 'OIHW', 'NCHW'))
        return out + bias[None, :, None, None]

    def _gn(v, G=4, eps=1e-5):
        B_, C_, H_, W_ = v.shape
        g = v.reshape(B_, G, C_ // G, H_, W_)
        m = jnp.mean(g, axis=(2, 3, 4), keepdims=True)
        s = jnp.var(g, axis=(2, 3, 4), keepdims=True)
        return ((g - m) / jnp.sqrt(s + eps)).reshape(v.shape)

    def _ln_c(v, eps=1e-6):
        m = jnp.mean(v, axis=1, keepdims=True)
        s = jnp.var(v, axis=1, keepdims=True)
        return (v - m) / jnp.sqrt(s + eps)

    def _ln_t(v, eps=1e-5):
        m = jnp.mean(v, axis=-1, keepdims=True)
        s = jnp.var(v, axis=-1, keepdims=True)
        return (v - m) / jnp.sqrt(s + eps)

    def _to_tokens(v):
        B_, C_, H_, W_ = v.shape
        return v.reshape(B_, C_, H_ * W_).transpose(0, 2, 1)
    def _from_tokens(t, like):
        B_, C_, H_, W_ = like.shape
        return t.transpose(0, 2, 1).reshape(B_, C_, H_, W_)

    x = x + _L0_conv_ref(_gn(x), L0_conv_weight, L0_conv_bias)
    x = x + _L1_conv_ref(_gn(x), L1_conv_weight, L1_conv_bias)
    return x


_drawn_inputs = setup_inputs


def setup_inputs(seed=0):
    import zlib

    import numpy as np

    out = dict(_drawn_inputs(seed))
    spreads = {}
    factors = {}
    for name, (base, spread) in spreads.items():
        noise = np.random.default_rng([zlib.crc32(name.encode()), seed]).standard_normal(out[name].shape)
        drawn = base * np.exp(spread * noise) if base else spread * noise
        out[name] = jnp.asarray(drawn.astype(out[name].dtype))
    for name, factor in factors.items():
        out[name] = (out[name] * factor).astype(out[name].dtype)
    return out
```

```python
from collections import namedtuple
from contextlib import ExitStack

import concourse.bass as bass
from concourse import mybir

F32 = mybir.dt.float32
F16 = mybir.dt.float16
I32 = mybir.dt.int32
ALU = mybir.AluOpType
ACT = mybir.ActivationFunctionType
AX_X = mybir.AxisListType.X

P = 128
C = 8
GROUPS = 4
ROWS_IN = P // C
ROWS_OUT = ROWS_IN - 2
TAPS = 3
BANK = 512
RING = 4
EPS = 1e-5
WEIGHT_TOP = 1024.0
KX = 18
KY = 21

Task = namedtuple("Task", "layer image tile edge q slot x_stage y_stage chunk")
Chunk = namedtuple("Chunk", "image index slot use ring")


def conv_preact_program(nc, x, weight0, weight1, bias0, bias1, avg_x, avg_x_rows, avg_y, avg_y_last,
                        edge_keep, out):
    B, _, H, W = x.shape
    HALVES = W // BANK
    TILES = -(-H // ROWS_OUT)
    LAST_ROWS = H - (TILES - 1) * ROWS_OUT
    LAST_K = 32
    CHUNK = 1024
    CHUNKS = C * H * W // P // CHUNK
    HEAD = 4
    LOOPED = (TILES - HEAD) // 2 - 2
    FIRST_LOOPED = CHUNKS // 4
    STAT_LOOPED = CHUNKS // 2
    assert LAST_ROWS + 2 == LAST_K // C and W == HALVES * BANK
    assert TILES % 4 == 2 and 4 + 4 * FIRST_LOOPED + 6 == TILES and STAT_LOOPED + 1 == LOOPED

    x_flat = x.rearrange("b c h w -> b (c h w)").rearrange("b (p f) -> b p f", p=P)
    y = nc.dram_tensor("y", [B, H, C, W], F32, kind="Internal").ap()


    def phase_q(b):
        return TILES // 4 + (2 * TILES // 4) * (b - 1)

    def task(q0, m, i, layer, image, tile, edge=None, x_stage=None, y_stage=(), chunk=None):
        return Task(layer, image, tile, edge, q0 + m // RING + i, m % RING, x_stage, y_stage, chunk)

    def walk_gather(eng, do_chunk):
        with eng.Fori(0, CHUNKS // RING) as i:
            for s in range(RING):
                do_chunk(Chunk(0, RING * i + s, s, i, RING))

    def walk_first(eng, do):
        for n in range(4):
            do(task(0, n, 0, 0, 0, n, "top" if n == 0 else None))
        with eng.Fori(0, FIRST_LOOPED) as i:
            for j in range(4):
                do(task(0, 4 + j, i, 0, 0, 4 + 4 * i + j,
                        chunk=Chunk(1, 4 * i + j, j, CHUNKS // RING + i, RING)))
        for n in range(TILES - 6, TILES):
            last = n == TILES - 1
            do(task(0, n, 0, 0, 0, n, "bottom" if last else None,
                    x_stage={TILES - 6: 0, TILES - 4: 1, TILES - 3: 2}.get(n),
                    y_stage=(0, 1, 2) if last else ()))

    def walk_middle(eng, do, b, with_stats):
        q0 = phase_q(b)

        def body(i, p, with_chunks, stages=()):
            for j in range(4):
                m, tile = 6 + 2 * p + j, p + j // 2 + 2 * i
                chunk = None
                if with_chunks and j % 2:
                    chunk = Chunk(b + 1, 2 * i + j // 2, j // 2,
                                  2 * (CHUNKS // RING) + STAT_LOOPED * (b - 1) + i, 2)
                edge = "top" if p + j == 0 else None
                last = j == 3 and p + 2 + HEAD == TILES
                x_stage = dict(stages).get(j)
                if j % 2 == 0:
                    do(task(q0, m, i, 1, b - 1, tile, edge, x_stage=x_stage, chunk=chunk))
                else:
                    do(task(q0, m, i, 0, b, tile + HEAD, "bottom" if last else None,
                            x_stage=x_stage, y_stage=(0,) if last else (), chunk=chunk))

        for k in range(HEAD):
            do(task(q0, 2 + k, 0, 0, b, k, "top" if k == 0 else None))
        body(0, 0, False)
        if with_stats:
            with eng.Fori(0, STAT_LOOPED) as i:
                body(i, 2, True)
            body(0, 2 + 2 * STAT_LOOPED, False, ((0, 0), (2, 1)))
            body(0, 4 + 2 * STAT_LOOPED, False, ((0, 2),))
        else:
            with eng.Fori(0, LOOPED) as i:
                body(i, 2, False)
            body(0, 2 + 2 * LOOPED, False)
        y_stages = {1: (1,), 3: (2,)} if with_stats else {0: (1,), 1: (2,)}
        for k in range(HEAD):
            tile = TILES - HEAD + k
            do(task(q0, 6 + 2 * (TILES - HEAD) + k, 0, 1, b - 1, tile,
                    "bottom" if k == HEAD - 1 else None, y_stage=y_stages.get(k, ())))

    def walk_last(eng, do):
        q0 = phase_q(B)
        for k in range(2):
            do(task(q0, 2 + k, 0, 1, B - 1, k, "top" if k == 0 else None))
        with eng.Fori(0, (TILES - 6) // 4) as i:
            for j in range(4):
                do(task(q0, 4 + j, i, 1, B - 1, 2 + 4 * i + j))
        for k in range(TILES - 4, TILES):
            do(task(q0, 2 + k, 0, 1, B - 1, k, "bottom" if k == TILES - 1 else None))

    def walk(eng, do):
        walk_first(eng, do)
        with eng.Fori(1, B - 1) as b:
            walk_middle(eng, do, b, True)
        walk_middle(eng, do, B - 1, False)
        walk_last(eng, do)

    def number(k):
        return 4 * k.q + k.slot

    def after(k, back):
        if isinstance(k.q, int) and 4 * k.q + k.slot - back < 0:
            return None
        return 4 * k.q + (k.slot - back + 1)

    TASKS = 2 * B * TILES

    with ExitStack() as ctx:
        def sb(name, shape, dt):
            return ctx.enter_context(nc.sbuf_tensor(name, shape, dt))

        def sem(name):
            return ctx.enter_context(nc.semaphore(name))

        x_in = sb("x_in", [P, RING, W], F32)
        x_hat = sb("x_hat", [P, 2, W], F32)
        resid = sb("resid", [P, RING, W], F32)
        high = sb("high", [P, RING, W + 2], F16)
        low = sb("low", [P, RING, W + 2], F16)
        y_out = sb("y_out", [P, RING, W], F32)
        chunks = sb("chunks", [P, RING, CHUNK], F32)
        x_moments = sb("x_moments", [P, CHUNKS * 2 * 6], F32)
        y_moments = sb("y_moments", [P, (TILES - 1) * HALVES * 6], F32)
        y_moments_last = sb("y_moments_last", [P, HALVES * 6], F32)
        band = sb("band", [P, 2, TAPS, P], F32)
        band_abs = sb("band_abs", [P, 2, TAPS * P], F32)
        w_high = sb("w_high", [P, 2, TAPS, P], F16)
        w_low = sb("w_low", [P, 2, TAPS, P], F16)
        w_max = sb("w_max", [P, 2], F32)
        w_max_all = sb("w_max_all", [P, 2], F32)
        w_pow2 = sb("w_pow2", [P, 2], F32)
        w_scale = sb("w_scale", [P, 2], F32)
        w_unscale = sb("w_unscale", [P, 2], F32)
        bias = sb("bias", [P, 2], F32)
        avg_x_sb = sb("avg_x_sb", [P, P], F32)
        avg_x_rows_sb = sb("avg_x_rows_sb", [P, P], F32)
        avg_y_sb = sb("avg_y_sb", [P, P], F32)
        avg_y_last_sb = sb("avg_y_last_sb", [P, P], F32)
        edge_keep_sb = sb("edge_keep_sb", [P, 2], F32)
        mv = [sb(f"mv{l}", [P, 2], F32) for l in range(2)]
        mv_last = sb("mv_last", [P, 2], F32)
        diff = [sb(f"diff{l}", [P, 2], F32) for l in range(2)]
        var_eps = [sb(f"var_eps{l}", [P, 1], F32) for l in range(2)]
        guess = [sb(f"guess{l}", [P, 2], F32) for l in range(2)]
        tmp = [sb(f"tmp{l}", [P, 2], F32) for l in range(2)]
        fresh = [sb(f"fresh{l}", [P, 6], F32) for l in range(2)]
        affine = [sb(f"affine{l}", [P, 6], F32) for l in range(2)]

        conv = ctx.enter_context(nc.psum_tensor("conv", [P, 2, HALVES, BANK], F32))
        stat = [ctx.enter_context(nc.psum_tensor(f"stat{l}", [P, BANK], F32)) for l in range(2)]

        consts_loaded = sem("consts_loaded")
        band_zeroed = sem("band_zeroed")
        bands_loaded = sem("bands_loaded")
        max_found = sem("max_found")
        max_shared = sem("max_shared")
        scale_step = sem("scale_step")
        weights_ready = sem("weights_ready")
        pads_zeroed = sem("pads_zeroed")
        loaded = [sem(f"loaded{s}") for s in range(RING)]
        edge_loaded = {(l, e): sem(f"edge_loaded_{l}_{e}") for l in range(2) for e in ("top", "bottom")}
        chunk_loaded = [sem(f"chunk_loaded{s}") for s in range(RING)]
        chunk_done = sem("chunk_done")
        x_hat_ready = sem("x_hat_ready")
        resid_ready = sem("resid_ready")
        high_ready = sem("high_ready")
        low_ready = sem("low_ready")
        conv_done = sem("conv_done")
        y_ready = sem("y_ready")
        y_moments_done = sem("y_moments_done")
        stored = [sem(f"stored{s}") for s in range(RING)]
        chain = [sem("x_chain"), sem("y_chain")]
        mean_summed = [sem("x_mean_summed"), sem("y_mean_summed")]
        var_summed = [sem("x_var_summed"), sem("y_var_summed")]
        params_ready = [sem("x_params_ready"), sem("y_params_ready")]
        params_taken = [sem("x_params_taken"), sem("y_params_taken")]

        block = ctx.enter_context(nc.Block())

        @block.sync
        def _(sp):
            wait_registers = [sp.alloc_register(f"wait_count{n}") for n in range(3)]

            def load_chunk(c):
                src = x_flat[c.image, :, bass.ds(c.index * CHUNK, CHUNK)]
                if not (isinstance(c.use, int) and c.use == 0):
                    sp.wait_ge(chunk_done, CHUNKS * c.image + c.index - c.ring + 1)
                sp.dma_start(chunks[:, c.slot, :], src).then_inc(chunk_loaded[c.slot], 16)

            for s in range(RING):
                load_chunk(Chunk(0, s, s, 0, RING))
            with sp.Fori(1, CHUNKS // RING) as i:
                for s in range(RING):
                    load_chunk(Chunk(0, RING * i + s, s, i, RING))

            def load_tile(k):
                if k.layer == 1 and k.edge == "top":
                    q0 = phase_q(k.image + 1)
                    final = isinstance(k.image, int) and k.image == B - 1
                    counts = (16 * (q0 + (0 if final else 1)), 16 * (q0 - (1 if final else 0)),
                              after(k, RING))
                    for register, count in zip(wait_registers, counts):
                        sp.reg_mov(register, count)
                    for s in range(RING):
                        sp.wait_ge(stored[s], wait_registers[s // 2])
                    sp.wait_ge(resid_ready, wait_registers[2])
                elif (done := after(k, RING)) is not None:
                    sp.wait_ge(resid_ready, done)

                def rows(first, n):
                    if k.layer == 0:
                        return x[k.image, :, bass.ds(first, n), :].rearrange("c r w -> r c w")
                    return y[k.image, bass.ds(first, n), :, :].rearrange("r c w -> (r c) w")

                if k.edge == "top":
                    sp.dma_start(x_in[C:P, k.slot, :], rows(0, ROWS_IN - 1)
                                 ).then_inc(loaded[k.slot], 16)
                    sp.dma_start(x_in[0:C, k.slot, :], rows(0, 1)
                                 ).then_inc(edge_loaded[k.layer, "top"], 16)
                elif k.edge == "bottom":
                    n = LAST_ROWS + 1
                    sp.dma_start(x_in[0:n * C, k.slot, :], rows(H - n, n)
                                 ).then_inc(loaded[k.slot], 16)
                    sp.dma_start(x_in[n * C:LAST_K, k.slot, :], rows(H - 1, 1)
                                 ).then_inc(edge_loaded[k.layer, "bottom"], 16)
                else:
                    sp.dma_start(x_in[:, k.slot, :], rows(k.tile * ROWS_OUT - 1, ROWS_IN)
                                 ).then_inc(loaded[k.slot], 16)

                if k.chunk is not None:
                    load_chunk(k.chunk)

            walk(sp, load_tile)

        @block.scalar
        def _(act):
            act.wait_ge(band_zeroed, 1)
            for l, weight in enumerate((weight0, weight1)):
                for r in range(1, ROWS_OUT + 1):
                    act.dma_start(band[(r - 1) * C:(r + 2) * C, l, :, r * C:(r + 1) * C],
                                  weight.rearrange("kh ci kw co -> (kh ci) kw co")
                                  ).then_inc(bands_loaded, 16)
            with nc.allow_non_contiguous_dma(reason="eight values of bias"):
                for l, b in enumerate((bias0, bias1)):
                    for r in range(ROWS_IN):
                        act.dma_start(bias[r * C:(r + 1) * C, l:l + 1], b).then_inc(consts_loaded, 16)
                act.dma_start(edge_keep_sb[:, :], edge_keep).then_inc(consts_loaded, 16)
            for dst, src in ((avg_x_sb, avg_x), (avg_x_rows_sb, avg_x_rows), (avg_y_sb, avg_y),
                             (avg_y_last_sb, avg_y_last)):
                act.dma_start(dst[:, :], src).then_inc(consts_loaded, 16)
            act.wait_ge(consts_loaded, 16 * (2 * ROWS_IN + 5))
            act.wait_ge(pads_zeroed, 2)

            def prepare(k):
                l = k.layer
                if k.edge == "top":
                    act.wait_ge(params_ready[l], k.image + 1)
                    act.copy(affine[l][:, :], fresh[l][:, :]).then_inc(params_taken[l], 1)
                    act.wait_ge(params_taken[l], k.image + 1)
                act.wait_ge(loaded[k.slot], 16 * (k.q + 1))
                if k.edge:
                    act.wait_ge(edge_loaded[l, k.edge], 16 * (k.image + 1))
                if (done := after(k, 2)) is not None:
                    act.wait_ge(low_ready, done)
                a = {None: 0, "top": 2, "bottom": 4}[k.edge]
                nc.scalar.activation(x_hat[:, k.slot % 2, :], x_in[:, k.slot, :], ACT.Identity,
                                     scale=affine[l][:, a:a + 1], bias=affine[l][:, a + 1:a + 2]
                                     ).then_inc(x_hat_ready, 1)
                if (done := after(k, RING)) is not None:
                    act.wait_ge(y_ready, done)
                nc.scalar.activation(resid[:, k.slot, :], x_in[:, k.slot, :], ACT.Identity,
                                     scale=1.0, bias=bias[:, l:l + 1]).then_inc(resid_ready, 1)
                act.wait_ge(x_hat_ready, number(k) + 1)
                act.copy(high[:, k.slot, 1:W + 1], x_hat[:, k.slot % 2, :]).then_inc(high_ready, 1)

            walk(act, prepare)

        @block.tensor
        def _(pe):
            def sum_mean(l, image):
                pe.wait_ge(chain[l], image * (KX, KY)[l] + 1 + l)
                if l == 0:
                    pe.matmul(stat[0][:, 0:1], avg_x_sb[:, :], mv[0][:, 0:1], start=True,
                              stop=True).then_inc(mean_summed[0], 1)
                else:
                    pe.matmul(stat[1][:, 0:1], avg_y_sb[:, :], mv[1][:, 0:1], start=True, stop=False)
                    pe.matmul(stat[1][:, 0:1], avg_y_last_sb[:, :], mv_last[:, 0:1], start=False,
                              stop=True).then_inc(mean_summed[1], 1)

            def sum_var(l, image):
                pe.wait_ge(chain[l], image * (KX, KY)[l] + 3 + 3 * l)
                if l == 0:
                    pe.matmul(stat[0][:, 2:4], avg_x_rows_sb[:, :], mv[0][:, :], start=True,
                              stop=True).then_inc(var_summed[0], 1)
                else:
                    pe.matmul(stat[1][:, 2:4], avg_y_sb[:, :], mv[1][:, :], start=True, stop=False)
                    pe.matmul(stat[1][:, 2:4], avg_y_last_sb[:, :], mv_last[:, :], start=False,
                              stop=True).then_inc(var_summed[1], 1)

            def convolve(k):
                l, ps, kk = k.layer, k.slot % 2, LAST_K if k.edge == "bottom" else P
                pe.wait_ge(high_ready, number(k) + 1)
                if (done := after(k, 2)) is not None:
                    pe.wait_ge(y_ready, done)
                for part, (w, v) in enumerate(((w_high, high), (w_low, high), (w_high, low))):
                    if part == 2:
                        pe.wait_ge(low_ready, number(k) + 1)
                    for kw in range(TAPS):
                        for half in range(HALVES):
                            last = pe.matmul(
                                conv[:, ps, half, :], w[0:kk, l, kw, :],
                                v[0:kk, k.slot, half * BANK + kw:half * BANK + kw + BANK],
                                start=(part == 0 and kw == 0), stop=(part == 2 and kw == TAPS - 1))
                last.then_inc(conv_done, 1)
                if k.x_stage == 1:
                    sum_mean(0, k.image + 1 if l == 0 else k.image + 2)
                if k.x_stage == 2:
                    sum_var(0, k.image + 1 if l == 0 else k.image + 2)
                for stage in k.y_stage:
                    image = k.image if l == 0 else k.image + 1
                    if stage == 1:
                        sum_mean(1, image)
                    if stage == 2:
                        sum_var(1, image)

            pe.wait_ge(consts_loaded, 16 * (2 * ROWS_IN + 5))
            sum_mean(0, 0)
            sum_var(0, 0)
            pe.wait_ge(weights_ready, 1)
            walk(pe, convolve)

        @block.vector
        def _(dve):
            nc.vector.memset(high[:, :, :], 0.0).then_inc(pads_zeroed, 1)
            nc.vector.memset(low[:, :, :], 0.0).then_inc(pads_zeroed, 1)
            nc.vector.memset(mv_last[:, :], 0.0).then_inc(scale_step, 1)
            steps = [1]

            def step(ins):
                steps[0] += 1
                ins.then_inc(scale_step, 1)
                dve.wait_ge(scale_step, steps[0])

            def scale_weights():
                dve.wait_ge(bands_loaded, 2 * ROWS_OUT * 16)
                step(nc.vector.tensor_scalar(
                    band_abs[:, :, :].bitcast(I32),
                    band[:, :, :, :].rearrange("p l k n -> p l (k n)").bitcast(I32),
                    0x7FFFFFFF, None, ALU.bitwise_and))
                for l in range(2):
                    nc.vector.reduce_max(w_max[:, l:l + 1], band_abs[:, l, :], AX_X
                                         ).then_inc(max_found, 1)
                dve.wait_ge(max_shared, 1)
                step(nc.vector.tensor_scalar(w_max[:, :], w_max_all[:, :], 2.0 ** -100, None, ALU.max))
                step(nc.vector.tensor_scalar(w_pow2[:, :].bitcast(I32), w_max[:, :].bitcast(I32),
                                             0x7F800000, None, ALU.bitwise_and))
                step(nc.vector.tensor_scalar(w_unscale[:, :], w_pow2[:, :], 1.0 / WEIGHT_TOP, None,
                                             ALU.mult))
                step(nc.vector.reciprocal(w_scale[:, :], w_unscale[:, :]))
                for l in range(2):
                    step(nc.vector.tensor_scalar(w_high[:, l, :, :], band[:, l, :, :],
                                                 w_scale[:, l:l + 1], None, ALU.mult))
                    last = nc.vector.scalar_tensor_tensor(
                        w_low[:, l, :, :], band[:, l, :, :], w_scale[:, l:l + 1], w_high[:, l, :, :],
                        ALU.mult, ALU.subtract)
                    if l == 0:
                        step(last)
                last.then_inc(weights_ready, 1)

            def gather(c):
                dve.wait_ge(chunk_loaded[c.slot], 16 * (c.use + 1))
                nc.vector.bn_stats(x_moments[:, bass.ds(c.index * 12, 6)], chunks[:, c.slot, 0:BANK])
                nc.vector.bn_stats(x_moments[:, bass.ds(c.index * 12 + 6, 6)],
                                   chunks[:, c.slot, BANK:2 * BANK]).then_inc(chunk_done, 1)

            def linker(l, image, start):
                at = [start]

                def link(ins):
                    at[0] += 1
                    ins.then_inc(chain[l], 1)
                    dve.wait_ge(chain[l], image * (KX, KY)[l] + at[0])
                return link

            def aggregate(l, image):
                link = linker(l, image, 0)
                if l == 0:
                    dve.wait_ge(chunk_done, CHUNKS * (image + 1))
                    nc.vector.memset(tmp[0][:, :], 0.0)
                    link(nc.vector.bn_aggr(mv[0][:, :], x_moments[:, :]))
                else:
                    dve.wait_ge(y_moments_done, TILES * (image + 1))
                    nc.vector.memset(tmp[1][:, :], 0.0)
                    nc.vector.bn_aggr(mv[1][:, :], y_moments[:, :]).then_inc(chain[1], 1)
                    nc.vector.bn_aggr(mv_last[0:LAST_K, :], y_moments_last[0:LAST_K, :]
                                      ).then_inc(chain[1], 1)
                    dve.wait_ge(chain[1], image * KY + 2)

            def distance(l, image):
                link = linker(l, image, 1 + l)
                dve.wait_ge(mean_summed[l], image + 1)
                for m, p in ((mv[l], P),) + (((mv_last, LAST_K),) if l else ()):
                    d = diff[l][0:p, 0:1] if p == P else diff[l][0:p, 1:2]
                    link(nc.vector.tensor_tensor(d, m[0:p, 0:1], stat[l][0:p, 0:1], ALU.subtract))
                    link(nc.vector.scalar_tensor_tensor(m[0:p, 1:2], d, d, m[0:p, 1:2],
                                                        ALU.mult, ALU.add))

            def finish(l, image):
                link = linker(l, image, 3 + 3 * l)
                dve.wait_ge(var_summed[l], image + 1)
                link(nc.vector.tensor_scalar(var_eps[l][:, :], stat[l][:, 3:4], EPS, None, ALU.add))
                g = guess[l]
                link(nc.vector.tensor_scalar(g[:, 0:1].bitcast(I32), var_eps[l][:, :].bitcast(I32),
                                             -0.5, float(0x5F3759DF), ALU.mult, ALU.add))
                for n in range(4):
                    a, b = g[:, n % 2:n % 2 + 1], g[:, 1 - n % 2:2 - n % 2]
                    link(nc.vector.scalar_tensor_tensor(tmp[l][:, 0:1], a, var_eps[l][:, 0:1], a,
                                                        ALU.mult, ALU.mult))
                    link(nc.vector.tensor_scalar(tmp[l][:, 1:2], tmp[l][:, 0:1], -0.5, 1.5,
                                                 ALU.mult, ALU.add))
                    if n < 3:
                        link(nc.vector.tensor_tensor(b, a, tmp[l][:, 1:2], ALU.mult))
                if not (isinstance(image, int) and image == 0):
                    dve.wait_ge(params_taken[l], image)
                link(nc.vector.tensor_tensor(fresh[l][:, 0:1], a, tmp[l][:, 1:2], ALU.mult))
                link(nc.vector.scalar_tensor_tensor(fresh[l][:, 1:2], stat[l][:, 2:3], -1.0,
                                                    fresh[l][:, 0:1], ALU.mult, ALU.mult))
                nc.vector.tensor_scalar(fresh[l][:, 2:4], fresh[l][:, 0:2], edge_keep_sb[:, 0:1],
                                        None, ALU.mult)
                nc.vector.tensor_scalar(fresh[l][:, 4:6], fresh[l][:, 0:2], edge_keep_sb[:, 1:2],
                                        None, ALU.mult).then_inc(params_ready[l], 1)

            def split_low(q, slot):
                dve.wait_ge(high_ready, 4 * q + slot + 1)
                nc.vector.tensor_tensor(low[:, slot, 1:W + 1], x_hat[:, slot % 2, :],
                                        high[:, slot, 1:W + 1], ALU.subtract).then_inc(low_ready, 1)

            def evacuate(k):
                l = k.layer
                dve.wait_ge(conv_done, number(k) + 1)
                if not (isinstance(k.q, int) and k.q == 0):
                    dve.wait_ge(stored[k.slot], 16 * k.q)
                nc.vector.scalar_tensor_tensor(
                    y_out[:, k.slot, :], conv[:, k.slot % 2, :, :].rearrange("p h n -> p (h n)"),
                    w_unscale[:, l:l + 1], resid[:, k.slot, :], ALU.mult, ALU.add
                    ).then_inc(y_ready, 1)
                if not (isinstance(k.q, int) and number(k) >= TASKS - 2):
                    split_low(k.q + (k.slot + 2) // RING, (k.slot + 2) % RING)
                if l == 0:
                    dve.wait_ge(y_ready, number(k) + 1)
                    for half in range(HALVES):
                        part = slice(half * BANK, (half + 1) * BANK)
                        if k.edge == "bottom":
                            last = nc.vector.bn_stats(y_moments_last[0:LAST_K, half * 6:half * 6 + 6],
                                                      y_out[0:LAST_K, k.slot, part])
                        else:
                            last = nc.vector.bn_stats(
                                y_moments[:, bass.ds((k.tile * HALVES + half) * 6, 6)],
                                y_out[:, k.slot, part])
                    last.then_inc(y_moments_done, 1)
                if k.chunk is not None:
                    gather(k.chunk)
                if k.x_stage is not None:
                    (aggregate, distance, finish)[k.x_stage](0, k.image + 1 if l == 0 else k.image + 2)
                for stage in k.y_stage:
                    (aggregate, distance, finish)[stage](1, k.image if l == 0 else k.image + 1)

            scale_weights()
            walk_gather(dve, gather)
            dve.wait_ge(consts_loaded, 16 * (2 * ROWS_IN + 5))
            aggregate(0, 0)
            distance(0, 0)
            finish(0, 0)
            split_low(0, 0)
            split_low(0, 1)
            walk(dve, evacuate)

        @block.gpsimd
        def _(pool):
            nc.gpsimd.memset(band[:, :, :, :], 0.0).then_inc(band_zeroed, 1)
            pool.wait_ge(max_found, 2)
            nc.gpsimd.partition_all_reduce(w_max_all[:, :], w_max[:, :], P,
                                           bass.bass_isa.ReduceOp.max).then_inc(max_shared, 1)

            def store(k):
                pool.wait_ge(y_ready, number(k) + 1)
                n = LAST_ROWS if k.edge == "bottom" else ROWS_OUT
                first = (TILES - 1) * ROWS_OUT if k.edge == "bottom" else k.tile * ROWS_OUT
                if k.layer == 0:
                    dst = y[k.image, bass.ds(first, n), :, :].rearrange("r c w -> (r c) w")
                else:
                    dst = out[k.image, :, bass.ds(first, n), :].rearrange("c r w -> r c w")
                pool.dma_start(dst, y_out[C:C + n * C, k.slot, :]).then_inc(stored[k.slot], 16)

            walk(pool, store)
            for s in range(RING):
                pool.wait_ge(stored[s], 16 * (TASKS // RING))


def constants(H, W):
    import numpy as np

    tiles = -(-H // ROWS_OUT)
    last_rows = H - (tiles - 1) * ROWS_OUT
    group_size = C // GROUPS * H * W
    p = np.arange(P)
    by_run = p // (P // GROUPS)
    row, by_tile = p // C, p % C // (C // GROUPS)
    inside = (row >= 1) & (row <= ROWS_OUT)
    inside_last = (row >= 1) & (row <= last_rows)
    same = (by_tile[:, None] == by_tile[None, :])
    return {
        "avg_x": (by_run[:, None] == by_run[None, :]) * (GROUPS / P),
        "avg_x_rows": (by_run[:, None] == by_tile[None, :]) * (GROUPS / P),
        "avg_y": same * inside[:, None] * ((tiles - 1) * W / group_size),
        "avg_y_last": same * inside_last[:, None] * (W / group_size),
        "edge_keep": np.stack([row >= 1, row <= last_rows], 1),
    }


def kernel(**inputs):
    import numpy as np
    import concourse.bacc as bacc
    from concourse.bass_utils import run_bass_kernel_spmd

    x = np.ascontiguousarray(inputs["x"])
    arrays = {"x": x}
    for l in range(2):
        arrays[f"weight{l}"] = np.ascontiguousarray(
            np.transpose(np.asarray(inputs[f"L{l}_conv_weight"]), (2, 1, 3, 0)))
        arrays[f"bias{l}"] = np.ascontiguousarray(np.asarray(inputs[f"L{l}_conv_bias"]).reshape(C, 1))
    for name, a in constants(x.shape[2], x.shape[3]).items():
        arrays[name] = np.ascontiguousarray(a.astype(np.float32))

    nc = bacc.Bacc("TRN2", target_bir_lowering=False, num_devices=1)
    aps = {n: nc.dram_tensor(n, a.shape, mybir.dt.from_np(a.dtype), kind="ExternalInput").ap()
           for n, a in arrays.items()}
    out = nc.dram_tensor("out", x.shape, F32, kind="ExternalOutput").ap()
    conv_preact_program(nc, out=out, **aps)
    r = run_bass_kernel_spmd(nc, [arrays], core_ids=[0])
    return r.results[0]["out"]
```

```python
from collections import namedtuple
from contextlib import ExitStack

import concourse.bass as bass
from concourse import mybir

F32 = mybir.dt.float32
F16 = mybir.dt.float16
I32 = mybir.dt.int32
ALU = mybir.AluOpType
ACT = mybir.ActivationFunctionType
AX_X = mybir.AxisListType.X

P = 128
C = 8
GROUPS = 4
ROWS_IN = P // C
ROWS_OUT = ROWS_IN - 2
TAPS = 3
BANK = 512
RING = 4
EPS = 1e-5
WEIGHT_TOP = 1024.0
KX = 15
KY = 18

Task = namedtuple("Task", "layer image tile edge cached seam q slot x_stage y_stage chunk")
Chunk = namedtuple("Chunk", "image index slot use ring")


def conv_preact_program(nc, x, weight0, weight1, bias0, bias1, avg_x, avg_y, avg_y_last,
                        edge_keep, out):
    B, _, H, W = x.shape
    HALVES = W // BANK
    TILES = -(-H // ROWS_OUT)
    LAST_ROWS = H - (TILES - 1) * ROWS_OUT
    LAST_K = 32
    CHUNKS = H // ROWS_IN
    HEAD = 4
    CACHED = 22
    SEAM = TILES - CACHED
    assert LAST_ROWS + 2 == LAST_K // C and W == HALVES * BANK
    assert TILES % 4 == 2 and SEAM % 4 == 0 and 4 * (CHUNKS // 4) + 10 == TILES

    y = nc.dram_tensor("y", [B, H, C, W], F32, kind="Internal").ap()


    def phase_q(b):
        return TILES // 4 + (2 * TILES // 4) * (b - 1)

    def task(q0, m, i, layer, image, tile, place, edge=None, x_stage=None, y_stage=(), chunk=None):
        return Task(layer, image, tile, edge, place != "dram", place == "seam",
                    q0 + m // RING + i, m % RING, x_stage, y_stage, chunk)

    def place_of(tile):
        return "dram" if tile < SEAM else "seam" if tile == SEAM else "sbuf"

    def walk_gather(eng, do_chunk, first, end):
        with eng.Fori(first, end) as i:
            for s in range(RING):
                do_chunk(Chunk(0, RING * i + s, s, i, RING))

    def walk_first(eng, do):
        def body(i, n):
            for j in range(4):
                c = Chunk(1, n - 4 + 4 * i + j, j, CHUNKS // RING + n // 4 - 1 + i, RING)
                do(task(0, n + j, i, 0, 0, n + 4 * i + j, place_of(n + j), chunk=c))

        for n in range(4):
            do(task(0, n, 0, 0, 0, n, "dram", "top" if n == 0 else None))
        with eng.Fori(0, SEAM // 4 - 1) as i:
            body(i, 4)
        body(0, SEAM)
        with eng.Fori(0, (TILES - 6 - SEAM) // 4 - 1) as i:
            body(i, SEAM + 4)
        for n in range(TILES - 6, TILES):
            last = n == TILES - 1
            do(task(0, n, 0, 0, 0, n, "sbuf", "bottom" if last else None,
                    x_stage={TILES - 6: 0, TILES - 4: 1, TILES - 3: 2}.get(n),
                    y_stage=(0,) if last else ()))
        walk_head(do, 1, {0: (1,), 1: (2,)})

    def walk_head(do, b, y_stages={}):
        for k in range(HEAD):
            do(task(phase_q(b), 2 + k, 0, 0, b, k, "dram", "top" if k == 0 else None,
                    y_stage=y_stages.get(k, ())))

    def walk_middle(eng, do, b, with_stats):
        q0 = phase_q(b)
        PAIRS = TILES - HEAD

        def body(i, p, x_stages=()):
            for j in range(4):
                pair = p + j // 2
                chunk = None
                if with_stats and j % 2 and 2 <= p < 2 + CHUNKS:
                    chunk = Chunk(b + 1, p - 2 + 2 * i + j // 2, j // 2,
                                  2 * (CHUNKS // RING) + (CHUNKS // 2) * (b - 1) + p // 2 - 1 + i, 2)
                x_stage = dict(x_stages).get(j) if with_stats else None
                if j % 2 == 0:
                    tile = TILES - 1 - pair
                    do(task(q0, 6 + 2 * p + j, i, 1, b - 1, tile - 2 * i, place_of(tile),
                            "bottom" if pair == 0 else None, x_stage=x_stage, chunk=chunk))
                else:
                    tile, last = pair + HEAD, pair == PAIRS - 1
                    do(task(q0, 6 + 2 * p + j, i, 0, b, tile + 2 * i, place_of(tile),
                            "bottom" if last else None, x_stage=x_stage,
                            y_stage=(0,) if last else (), chunk=chunk))

        def bodies(p, end):
            with eng.Fori(0, (end - p) // 2) as i:
                body(i, p)

        body(0, 0)
        bodies(2, CACHED - 2)
        body(0, CACHED - 2)
        bodies(CACHED, SEAM - HEAD)
        body(0, SEAM - HEAD)
        bodies(SEAM - HEAD + 2, PAIRS - 4)
        body(0, PAIRS - 4, ((0, 0), (2, 1)))
        body(0, PAIRS - 2, ((0, 2),))
        y_stages = {1: (1,), 3: (2,)} if with_stats else {0: (1,), 1: (2,)}
        for k in range(HEAD):
            do(task(q0, 6 + 2 * PAIRS + k, 0, 1, b - 1, HEAD - 1 - k, "dram",
                    "top" if k == HEAD - 1 else None, y_stage=y_stages.get(k, ())))
        if with_stats:
            walk_head(do, b + 1)

    def walk_last(eng, do):
        q0 = phase_q(B)

        def body(i, k, n=4):
            for k in range(k, k + n):
                tile = TILES - 1 - k
                do(task(q0, 2 + k, i, 1, B - 1, tile - 4 * i, place_of(tile),
                        {TILES - 1: "bottom", 0: "top"}.get(tile)))

        body(0, 0, 2)
        with eng.Fori(0, (CACHED - 6) // 4) as i:
            body(i, 2)
        body(0, CACHED - 4)
        with eng.Fori(0, (SEAM - 4) // 4) as i:
            body(i, CACHED)
        body(0, TILES - 4)

    def walk(eng, do):
        walk_first(eng, do)
        with eng.Fori(1, B - 1) as b:
            walk_middle(eng, do, b, True)
        walk_middle(eng, do, B - 1, False)
        walk_last(eng, do)

    def number(k):
        return 4 * k.q + k.slot

    def after(k, back):
        if isinstance(k.q, int) and 4 * k.q + k.slot - back < 0:
            return None
        return 4 * k.q + (k.slot - back + 1)

    def y_image(k, stage):
        if k.layer == 1:
            return k.image + 1
        return k.image - (stage > 0)

    def helped(k):
        return (k.layer == 0 and isinstance(k.image, int) and k.image == 0
                and not (isinstance(k.tile, int) and k.tile >= TILES - 2))

    TASKS = 2 * B * TILES

    with ExitStack() as ctx:
        def sb(name, shape, dt):
            return ctx.enter_context(nc.sbuf_tensor(name, shape, dt))

        def sem(name):
            return ctx.enter_context(nc.semaphore(name))

        x_in = sb("x_in", [P, RING, W], F32)
        x_hat = sb("x_hat", [P, 2, W], F32)
        resid = sb("resid", [P, RING, W], F32)
        high = sb("high", [P, RING, W + 2], F16)
        low = sb("low", [P, RING, W + 2], F16)
        y_out = sb("y_out", [P, RING, W], F32)
        y_cache = sb("y_cache", [P, CACHED * W], F32)
        chunks = sb("chunks", [P, RING, W], F32)
        x_moments = sb("x_moments", [P, CHUNKS * 2 * 6], F32)
        y_moments = sb("y_moments", [P, (TILES - 1) * HALVES * 6], F32)
        y_moments_last = sb("y_moments_last", [P, HALVES * 6], F32)
        band = sb("band", [P, 2, TAPS, P], F32)
        band_abs = sb("band_abs", [P, 2, TAPS * P], F32)
        w_high = sb("w_high", [P, 2, TAPS, P], F16)
        w_low = sb("w_low", [P, 2, TAPS, P], F16)
        w_max = sb("w_max", [P, 2], F32)
        w_max_all = sb("w_max_all", [P, 2], F32)
        w_pow2 = sb("w_pow2", [P, 2], F32)
        w_scale = sb("w_scale", [P, 2], F32)
        w_unscale = sb("w_unscale", [P, 2], F32)
        bias = sb("bias", [P, 2], F32)
        avg_x_sb = sb("avg_x_sb", [P, P], F32)
        avg_y_sb = sb("avg_y_sb", [P, P], F32)
        avg_y_last_sb = sb("avg_y_last_sb", [P, P], F32)
        edge_keep_sb = sb("edge_keep_sb", [P, 2], F32)
        mv = [sb(f"mv{l}", [P, 2], F32) for l in range(2)]
        mv_last = sb("mv_last", [P, 2], F32)
        diff = [sb(f"diff{l}", [P, 2], F32) for l in range(2)]
        var_eps = [sb(f"var_eps{l}", [P, 1], F32) for l in range(2)]
        guess = [sb(f"guess{l}", [P, 2], F32) for l in range(2)]
        tmp = [sb(f"tmp{l}", [P, 2], F32) for l in range(2)]
        fresh = [sb(f"fresh{l}", [P, 6], F32) for l in range(2)]
        affine = [sb(f"affine{l}", [P, 6], F32) for l in range(2)]

        conv = ctx.enter_context(nc.psum_tensor("conv", [P, 2, HALVES, BANK], F32))
        stat = [ctx.enter_context(nc.psum_tensor(f"stat{l}", [P, BANK], F32)) for l in range(2)]

        consts_loaded = sem("consts_loaded")
        band_zeroed = sem("band_zeroed")
        bands_loaded = sem("bands_loaded")
        max_found = sem("max_found")
        max_shared = sem("max_shared")
        scale_step = sem("scale_step")
        weights_ready = sem("weights_ready")
        pads_zeroed = sem("pads_zeroed")
        loaded = [sem(f"loaded{s}") for s in range(RING)]
        edge_loaded = {(l, e): sem(f"edge_loaded_{l}_{e}")
                       for l, e in ((0, "top"), (0, "bottom"), (1, "top"))}
        chunk_loaded = [sem(f"chunk_loaded{s}") for s in range(RING)]
        chunk_done = sem("chunk_done")
        x_hat_ready = sem("x_hat_ready")
        high_ready = sem("high_ready")
        low_ready = sem("low_ready")
        conv_done = sem("conv_done")
        y_ready = sem("y_ready")
        y_moments_done = sem("y_moments_done")
        stored = [sem(f"stored{s}") for s in range(RING)]
        chain = [sem("x_chain"), sem("y_chain")]
        mean_summed = [sem("x_mean_summed"), sem("y_mean_summed")]
        var_summed = [sem("x_var_summed"), sem("y_var_summed")]
        params_ready = [sem("x_params_ready"), sem("y_params_ready")]
        params_taken = [sem("x_params_taken"), sem("y_params_taken")]

        def split_low(eng, q, slot):
            eng.wait_ge(high_ready, 4 * q + slot + 1)
            eng.tensor_tensor(low[:, slot, 1:W + 1], x_hat[:, slot % 2, :],
                              high[:, slot, 1:W + 1], ALU.subtract).then_inc(low_ready, 1)

        def in_cache(tile, first, end):
            return y_cache[first:end, bass.ds((tile - SEAM) * W, W)]

        block = ctx.enter_context(nc.Block())

        @block.sync
        def _(sp):
            place_register = sp.alloc_register("place")
            wait_registers = [sp.alloc_register(f"wait_count{n}") for n in range(3)]

            def load_chunk(c):
                src = x[c.image, :, bass.ds(c.index * ROWS_IN, ROWS_IN), :].rearrange("c r w -> r c w")
                if not (isinstance(c.use, int) and c.use == 0):
                    sp.wait_ge(chunk_done, CHUNKS * c.image + c.index - c.ring + 1)
                sp.dma_start(chunks[:, c.slot, :], src).then_inc(chunk_loaded[c.slot], 16)

            for s in range(RING):
                load_chunk(Chunk(0, s, s, 0, RING))
            walk_gather(sp, load_chunk, 1, CHUNKS // RING)

            def held(value, least, most):
                if isinstance(value, int):
                    return value
                sp.reg_mov(place_register, value)
                return sp.snap(place_register, min_val=least, max_val=most)

            def load_tile(k):
                if k.layer == 1 and k.cached:
                    offset = held((k.tile - SEAM) * W, W, (CACHED - 1) * W)
                elif k.edge is None:
                    first_row = held(k.tile * ROWS_OUT - 1, 0, H - ROWS_IN)
                if k.layer == 1 and k.edge == "bottom":
                    q0 = phase_q(k.image + 1)
                    final = isinstance(k.image, int) and k.image == B - 1
                    counts = (16 * (q0 + (0 if final else 1)), 16 * (q0 - (1 if final else 0)),
                              TILES * (k.image + 1))
                    for register, count in zip(wait_registers, counts):
                        sp.reg_mov(register, count)
                    for s in range(RING):
                        sp.wait_ge(stored[s], wait_registers[s // 2])
                    sp.wait_ge(y_moments_done, wait_registers[2])
                elif (done := after(k, RING)) is not None:
                    sp.wait_ge(high_ready, done)

                def rows(first, n):
                    if k.layer == 0:
                        return x[k.image, :, bass.ds(first, n), :].rearrange("c r w -> r c w")
                    return y[k.image, bass.ds(first, n), :, :].rearrange("r c w -> (r c) w")

                if k.layer == 1 and k.cached:
                    above = (rows(SEAM * ROWS_OUT - 1, 1) if k.seam
                             else y_cache[P - 2 * C:P - C, bass.ds(offset - W, W)])
                    sp.dma_start(y_cache[0:C, bass.ds(offset, W)], above
                                 ).then_inc(loaded[k.slot], 16)
                elif k.edge == "top":
                    sp.dma_start(x_in[0:C, k.slot, :], rows(1, 1)
                                 ).then_inc(edge_loaded[k.layer, "top"], 16)
                    sp.dma_start(x_in[C:P, k.slot, :], rows(0, ROWS_IN - 1)
                                 ).then_inc(loaded[k.slot], 16)
                elif k.edge == "bottom":
                    n = LAST_ROWS + 1
                    sp.dma_start(x_in[0:n * C, k.slot, :], rows(H - n, n)
                                 ).then_inc(loaded[k.slot], 16)
                    sp.dma_start(x_in[n * C:LAST_K, k.slot, :], rows(H - 1, 1)
                                 ).then_inc(edge_loaded[k.layer, "bottom"], 16)
                else:
                    sp.dma_start(x_in[:, k.slot, :], rows(first_row, ROWS_IN)
                                 ).then_inc(loaded[k.slot], 16)

                if k.chunk is not None:
                    load_chunk(k.chunk)

            walk(sp, load_tile)

        @block.scalar
        def _(act):
            act.wait_ge(band_zeroed, 1)
            for l, weight in enumerate((weight0, weight1)):
                for r in range(1, ROWS_OUT + 1):
                    act.dma_start(band[(r - 1) * C:(r + 2) * C, l, :, r * C:(r + 1) * C],
                                  weight.rearrange("kh ci kw co -> (kh ci) kw co")
                                  ).then_inc(bands_loaded, 16)
            with nc.allow_non_contiguous_dma(reason="eight values of bias"):
                for l, b in enumerate((bias0, bias1)):
                    for r in range(ROWS_IN):
                        act.dma_start(bias[r * C:(r + 1) * C, l:l + 1], b).then_inc(consts_loaded, 16)
                act.dma_start(edge_keep_sb[:, :], edge_keep).then_inc(consts_loaded, 16)
            for dst, src in ((avg_x_sb, avg_x), (avg_y_sb, avg_y),
                             (avg_y_last_sb, avg_y_last)):
                act.dma_start(dst[:, :], src).then_inc(consts_loaded, 16)
            act.wait_ge(consts_loaded, 16 * (2 * ROWS_IN + 4))
            act.wait_ge(pads_zeroed, 2)

            def prepare(k):
                l = k.layer
                src = in_cache(k.tile, 0, P) if l == 1 and k.cached else x_in[:, k.slot, :]

                def add_bias():
                    nc.scalar.activation(resid[:, k.slot, :], src, ACT.Identity,
                                         scale=1.0, bias=bias[:, l:l + 1])

                act.wait_ge(loaded[k.slot], 16 * (k.q + 1))
                if (l, k.edge) in edge_loaded:
                    act.wait_ge(edge_loaded[l, k.edge], 16 * (k.image + 1))
                if (done := after(k, RING)) is not None:
                    act.wait_ge(y_ready, done)
                first = k.edge == ("top", "bottom")[l]
                if first:
                    add_bias()
                    act.wait_ge(params_ready[l], k.image + 1)
                    act.copy(affine[l][:, :], fresh[l][:, :]).then_inc(params_taken[l], 1)
                    act.wait_ge(params_taken[l], k.image + 1)
                if (done := after(k, 2)) is not None:
                    act.wait_ge(low_ready, done)
                a = {None: 0, "top": 2, "bottom": 4}[k.edge]
                nc.scalar.activation(x_hat[:, k.slot % 2, :], src, ACT.Identity,
                                     scale=affine[l][:, a:a + 1], bias=affine[l][:, a + 1:a + 2]
                                     ).then_inc(x_hat_ready, 1)
                if not first:
                    add_bias()
                act.wait_ge(x_hat_ready, number(k) + 1)
                act.copy(high[:, k.slot, 1:W + 1], x_hat[:, k.slot % 2, :]).then_inc(high_ready, 1)

            walk(act, prepare)

        @block.tensor
        def _(pe):
            def sum_mean(l, image):
                pe.wait_ge(chain[l], image * (KX, KY)[l] + 1 + l)
                if l == 0:
                    pe.matmul(stat[0][:, 0:1], avg_x_sb[:, :], mv[0][:, 0:1], start=True,
                              stop=True).then_inc(mean_summed[0], 1)
                else:
                    pe.matmul(stat[1][:, 0:1], avg_y_sb[:, :], mv[1][:, 0:1], start=True, stop=False)
                    pe.matmul(stat[1][:, 0:1], avg_y_last_sb[:, :], mv_last[:, 0:1], start=False,
                              stop=True).then_inc(mean_summed[1], 1)

            def sum_var(l, image):
                pe.wait_ge(chain[l], image * (KX, KY)[l] + 3 + 3 * l)
                if l == 0:
                    pe.matmul(stat[0][:, 2:4], avg_x_sb[:, :], mv[0][:, :], start=True,
                              stop=True).then_inc(var_summed[0], 1)
                else:
                    pe.matmul(stat[1][:, 2:4], avg_y_sb[:, :], mv[1][:, :], start=True, stop=False)
                    pe.matmul(stat[1][:, 2:4], avg_y_last_sb[:, :], mv_last[:, :], start=False,
                              stop=True).then_inc(var_summed[1], 1)

            def convolve(k):
                l, ps, kk = k.layer, k.slot % 2, LAST_K if k.edge == "bottom" else P
                pe.wait_ge(high_ready, number(k) + 1)
                if (done := after(k, 2)) is not None:
                    pe.wait_ge(y_ready, done)
                for part, (w, v) in enumerate(((w_high, high), (w_low, high), (w_high, low))):
                    if part == 2:
                        pe.wait_ge(low_ready, number(k) + 1)
                    for kw in range(TAPS):
                        for half in range(HALVES):
                            last = pe.matmul(
                                conv[:, ps, half, :], w[0:kk, l, kw, :],
                                v[0:kk, k.slot, half * BANK + kw:half * BANK + kw + BANK],
                                start=(part == 0 and kw == 0), stop=(part == 2 and kw == TAPS - 1))
                last.then_inc(conv_done, 1)
                if k.x_stage == 1:
                    sum_mean(0, k.image + 1 if l == 0 else k.image + 2)
                if k.x_stage == 2:
                    sum_var(0, k.image + 1 if l == 0 else k.image + 2)
                for stage in k.y_stage:
                    if stage == 1:
                        sum_mean(1, y_image(k, stage))
                    if stage == 2:
                        sum_var(1, y_image(k, stage))

            pe.wait_ge(consts_loaded, 16 * (2 * ROWS_IN + 4))
            sum_mean(0, 0)
            sum_var(0, 0)
            pe.wait_ge(weights_ready, 1)
            walk(pe, convolve)

        @block.vector
        def _(dve):
            nc.vector.memset(high[:, :, :], 0.0).then_inc(pads_zeroed, 1)
            nc.vector.memset(low[:, :, :], 0.0).then_inc(pads_zeroed, 1)
            nc.vector.memset(mv_last[:, :], 0.0).then_inc(scale_step, 1)
            steps = [1]

            def step(ins):
                steps[0] += 1
                ins.then_inc(scale_step, 1)
                dve.wait_ge(scale_step, steps[0])

            def scale_weights():
                dve.wait_ge(bands_loaded, 2 * ROWS_OUT * 16)
                step(nc.vector.tensor_scalar(
                    band_abs[:, :, :].bitcast(I32),
                    band[:, :, :, :].rearrange("p l k n -> p l (k n)").bitcast(I32),
                    0x7FFFFFFF, None, ALU.bitwise_and))
                for l in range(2):
                    nc.vector.reduce_max(w_max[:, l:l + 1], band_abs[:, l, :], AX_X
                                         ).then_inc(max_found, 1)
                dve.wait_ge(max_shared, 1)
                step(nc.vector.tensor_scalar(w_max[:, :], w_max_all[:, :], 2.0 ** -100, None, ALU.max))
                step(nc.vector.tensor_scalar(w_pow2[:, :].bitcast(I32), w_max[:, :].bitcast(I32),
                                             0x7F800000, None, ALU.bitwise_and))
                step(nc.vector.tensor_scalar(w_unscale[:, :], w_pow2[:, :], 1.0 / WEIGHT_TOP, None,
                                             ALU.mult))
                step(nc.vector.reciprocal(w_scale[:, :], w_unscale[:, :]))
                for l in range(2):
                    step(nc.vector.tensor_scalar(w_high[:, l, :, :], band[:, l, :, :],
                                                 w_scale[:, l:l + 1], None, ALU.mult))
                    last = nc.vector.scalar_tensor_tensor(
                        w_low[:, l, :, :], band[:, l, :, :], w_scale[:, l:l + 1], w_high[:, l, :, :],
                        ALU.mult, ALU.subtract)
                    if l == 0:
                        step(last)
                last.then_inc(weights_ready, 1)

            def gather(c):
                dve.wait_ge(chunk_loaded[c.slot], 16 * (c.use + 1))
                nc.vector.bn_stats(x_moments[:, bass.ds(c.index * 12, 6)], chunks[:, c.slot, 0:BANK])
                nc.vector.bn_stats(x_moments[:, bass.ds(c.index * 12 + 6, 6)],
                                   chunks[:, c.slot, BANK:2 * BANK]).then_inc(chunk_done, 1)

            def linker(l, image, start):
                at = [start]

                def link(ins):
                    at[0] += 1
                    ins.then_inc(chain[l], 1)
                    dve.wait_ge(chain[l], image * (KX, KY)[l] + at[0])
                return link

            def aggregate(l, image):
                link = linker(l, image, 0)
                if l == 0:
                    dve.wait_ge(chunk_done, CHUNKS * (image + 1))
                    nc.vector.memset(tmp[0][:, :], 0.0)
                    link(nc.vector.bn_aggr(mv[0][:, :], x_moments[:, :]))
                else:
                    dve.wait_ge(y_moments_done, TILES * (image + 1))
                    nc.vector.memset(tmp[1][:, :], 0.0)
                    nc.vector.bn_aggr(mv[1][:, :], y_moments[:, :]).then_inc(chain[1], 1)
                    nc.vector.bn_aggr(mv_last[0:LAST_K, :], y_moments_last[0:LAST_K, :]
                                      ).then_inc(chain[1], 1)
                    dve.wait_ge(chain[1], image * KY + 2)

            def distance(l, image):
                link = linker(l, image, 1 + l)
                dve.wait_ge(mean_summed[l], image + 1)
                for m, p in ((mv[l], P),) + (((mv_last, LAST_K),) if l else ()):
                    d = diff[l][0:p, 0:1] if p == P else diff[l][0:p, 1:2]
                    link(nc.vector.tensor_tensor(d, m[0:p, 0:1], stat[l][0:p, 0:1], ALU.subtract))
                    link(nc.vector.scalar_tensor_tensor(m[0:p, 1:2], d, d, m[0:p, 1:2],
                                                        ALU.mult, ALU.add))

            def finish(l, image):
                link = linker(l, image, 3 + 3 * l)
                dve.wait_ge(var_summed[l], image + 1)
                link(nc.vector.tensor_scalar(var_eps[l][:, :], stat[l][:, 3:4], EPS, None, ALU.add))
                g = guess[l]
                link(nc.vector.tensor_scalar(g[:, 0:1].bitcast(I32), var_eps[l][:, :].bitcast(I32),
                                             -0.5, float(0x5F3759DF), ALU.mult, ALU.add))
                for n in range(3):
                    a, b = g[:, n % 2:n % 2 + 1], g[:, 1 - n % 2:2 - n % 2]
                    link(nc.vector.scalar_tensor_tensor(tmp[l][:, 0:1], a, var_eps[l][:, 0:1], a,
                                                        ALU.mult, ALU.mult))
                    link(nc.vector.tensor_scalar(tmp[l][:, 1:2], tmp[l][:, 0:1], -0.5, 1.5,
                                                 ALU.mult, ALU.add))
                    if n < 2:
                        link(nc.vector.tensor_tensor(b, a, tmp[l][:, 1:2], ALU.mult))
                if not (isinstance(image, int) and image == 0):
                    dve.wait_ge(params_taken[l], image)
                link(nc.vector.tensor_tensor(fresh[l][:, 0:1], a, tmp[l][:, 1:2], ALU.mult))
                link(nc.vector.scalar_tensor_tensor(fresh[l][:, 1:2], stat[l][:, 2:3], -1.0,
                                                    fresh[l][:, 0:1], ALU.mult, ALU.mult))
                nc.vector.tensor_scalar(fresh[l][:, 2:4], fresh[l][:, 0:2], edge_keep_sb[:, 0:1],
                                        None, ALU.mult)
                nc.vector.tensor_scalar(fresh[l][:, 4:6], fresh[l][:, 0:2], edge_keep_sb[:, 1:2],
                                        None, ALU.mult).then_inc(params_ready[l], 1)

            def evacuate(k):
                l = k.layer
                dve.wait_ge(conv_done, number(k) + 1)
                if l == 0 and k.cached:
                    dst = in_cache(k.tile, 0, P)
                else:
                    dst = y_out[:, k.slot, :]
                    if not (isinstance(k.q, int) and k.q == 0):
                        dve.wait_ge(stored[k.slot], 16 * k.q)
                nc.vector.scalar_tensor_tensor(
                    dst, conv[:, k.slot % 2, :, :].rearrange("p h n -> p (h n)"),
                    w_unscale[:, l:l + 1], resid[:, k.slot, :], ALU.mult, ALU.add
                    ).then_inc(y_ready, 1)
                known = isinstance(k.q, int) and number(k) + 2
                if known == TILES:
                    dve.wait_ge(low_ready, TILES)
                if not helped(k) and not (known and known >= TASKS):
                    split_low(nc.vector, k.q + (k.slot + 2) // RING, (k.slot + 2) % RING)
                if l == 0:
                    dve.wait_ge(y_ready, number(k) + 1)
                    for half in range(HALVES):
                        rows = LAST_K if k.edge == "bottom" else P
                        if k.cached:
                            src = y_cache[0:rows, bass.ds((k.tile - SEAM) * W + half * BANK, BANK)]
                        else:
                            src = y_out[:, k.slot, half * BANK:(half + 1) * BANK]
                        if k.edge == "bottom":
                            last = nc.vector.bn_stats(y_moments_last[0:LAST_K, half * 6:half * 6 + 6],
                                                      src)
                        else:
                            last = nc.vector.bn_stats(
                                y_moments[:, bass.ds((k.tile * HALVES + half) * 6, 6)], src)
                    last.then_inc(y_moments_done, 1)
                if k.chunk is not None:
                    gather(k.chunk)
                if k.x_stage is not None:
                    (aggregate, distance, finish)[k.x_stage](0, k.image + 1 if l == 0 else k.image + 2)
                for stage in k.y_stage:
                    (aggregate, distance, finish)[stage](1, y_image(k, stage))

            walk_gather(dve, gather, 0, CHUNKS // RING - 2)
            scale_weights()
            walk_gather(dve, gather, CHUNKS // RING - 2, CHUNKS // RING)
            dve.wait_ge(consts_loaded, 16 * (2 * ROWS_IN + 4))
            aggregate(0, 0)
            distance(0, 0)
            finish(0, 0)
            walk(dve, evacuate)

        @block.gpsimd
        def _(pool):
            nc.gpsimd.memset(band[:, :, :, :], 0.0).then_inc(band_zeroed, 1)
            pool.wait_ge(max_found, 2)
            nc.gpsimd.partition_all_reduce(w_max_all[:, :], w_max[:, :], P,
                                           bass.bass_isa.ReduceOp.max).then_inc(max_shared, 1)

            tile_register = pool.alloc_register("tile")

            def store(k):
                if helped(k):
                    if (done := after(k, 2)) is not None:
                        pool.wait_ge(conv_done, done)
                    split_low(nc.gpsimd, k.q + (k.slot + 2) // RING, (k.slot + 2) % RING)
                stays = k.layer == 0 and k.cached
                tile = k.tile
                if not isinstance(tile, int) or (stays and not isinstance(k.q, int)):
                    pool.reg_mov(tile_register, tile)
                    tile = pool.snap(tile_register, min_val=SEAM + (not k.seam) if stays else 0,
                                     max_val=TILES - 1 if k.edge == "bottom" else TILES - 2)
                if stays:
                    pool.wait_ge(y_moments_done, TILES * k.image + k.tile)
                    pool.wait_ge(y_ready, number(k) + 1)
                    dst = (y[k.image, SEAM * ROWS_OUT, :, :] if k.seam
                           else in_cache(tile - 1, P - C, P))
                    pool.dma_start(dst, in_cache(tile, C, 2 * C)).then_inc(stored[k.slot], 16)
                    return
                pool.wait_ge(y_ready, number(k) + 1)
                n = LAST_ROWS if k.edge == "bottom" else ROWS_OUT
                if k.layer == 0:
                    dst = y[k.image, bass.ds(tile * ROWS_OUT, n), :, :].rearrange("r c w -> (r c) w")
                else:
                    dst = out[k.image, :, bass.ds(tile * ROWS_OUT, n), :].rearrange("c r w -> r c w")
                pool.dma_start(dst, y_out[C:C + n * C, k.slot, :]).then_inc(stored[k.slot], 16)

            pool.wait_ge(pads_zeroed, 2)
            split_low(nc.gpsimd, 0, 0)
            split_low(nc.gpsimd, 0, 1)
            walk(pool, store)
            for s in range(RING):
                pool.wait_ge(stored[s], 16 * (TASKS // RING))


def constants(H, W):
    import numpy as np

    tiles = -(-H // ROWS_OUT)
    last_rows = H - (tiles - 1) * ROWS_OUT
    group_size = C // GROUPS * H * W
    p = np.arange(P)
    row, group = p // C, p % C // (C // GROUPS)
    inside = (row >= 1) & (row <= ROWS_OUT)
    inside_last = (row >= 1) & (row <= last_rows)
    same = group[:, None] == group[None, :]
    return {
        "avg_x": same * (GROUPS / P),
        "avg_y": same * inside[:, None] * ((tiles - 1) * W / group_size),
        "avg_y_last": same * inside_last[:, None] * (W / group_size),
        "edge_keep": np.stack([row >= 1, row <= last_rows], 1),
    }


def kernel(**inputs):
    import numpy as np
    import concourse.bacc as bacc
    from concourse.bass_utils import run_bass_kernel_spmd

    x = np.ascontiguousarray(inputs["x"])
    arrays = {"x": x}
    for l in range(2):
        arrays[f"weight{l}"] = np.ascontiguousarray(
            np.transpose(np.asarray(inputs[f"L{l}_conv_weight"]), (2, 1, 3, 0)))
        arrays[f"bias{l}"] = np.ascontiguousarray(np.asarray(inputs[f"L{l}_conv_bias"]).reshape(C, 1))
    for name, a in constants(x.shape[2], x.shape[3]).items():
        arrays[name] = np.ascontiguousarray(a.astype(np.float32))

    nc = bacc.Bacc("TRN2", target_bir_lowering=False, num_devices=1)
    aps = {n: nc.dram_tensor(n, a.shape, mybir.dt.from_np(a.dtype), kind="ExternalInput").ap()
           for n, a in arrays.items()}
    out = nc.dram_tensor("out", x.shape, F32, kind="ExternalOutput").ap()
    conv_preact_program(nc, out=out, **aps)
    r = run_bass_kernel_spmd(nc, [arrays], core_ids=[0])
    return r.results[0]["out"]
```

```python
from collections import namedtuple
from contextlib import ExitStack

import concourse.bass as bass
from concourse import mybir

F32 = mybir.dt.float32
F16 = mybir.dt.float16
I32 = mybir.dt.int32
ALU = mybir.AluOpType
ACT = mybir.ActivationFunctionType
AX_X = mybir.AxisListType.X

P = 128
C = 8
GROUPS = 4
ROWS_IN = P // C
ROWS_OUT = ROWS_IN - 2
TAPS = 3
BANK = 512
RING = 4
LAST_K = 32
EPS = 1e-5
WEIGHT_TOP = 1024.0
KX = 15
KY = 18

Task = namedtuple("Task", "layer image tile edge cached seam q slot x_stage y_stage chunk then_last")
Chunk = namedtuple("Chunk", "image index slot use ring")


def conv_preact_program(nc, x, weight0, weight1, bias0, bias1, avg_x, avg_y, avg_y_last,
                        edge_keep, out):
    B, _, H, W = x.shape
    HALVES = W // BANK
    TILES = -(-H // ROWS_OUT)
    LAST_ROWS = H - (TILES - 1) * ROWS_OUT
    STACK = 3
    CHUNKS = H // ROWS_IN
    FIRST_RING = 8
    HEAD = 4
    CACHED = 22
    SEAM = TILES - CACHED
    assert LAST_ROWS + 2 == LAST_K // C and W == HALVES * BANK
    assert TILES % 4 == 2 and SEAM % 4 == 0 and CHUNKS % FIRST_RING == 0
    assert SEAM + 4 < CHUNKS < TILES - 4

    y = nc.dram_tensor("y", [B, H, C, W], F32, kind="Internal").ap()


    def phase_q(b):
        return TILES // 4 + (2 * TILES // 4) * (b - 1)

    def task(q0, m, i, layer, image, tile, place, edge=None, x_stage=None, y_stage=(), chunk=None,
             then_last=False):
        return Task(layer, image, tile, edge, place != "dram", place == "seam",
                    q0 + m // RING + i, m % RING, x_stage, y_stage, chunk, then_last)

    def place_of(tile):
        return "dram" if tile < SEAM else "seam" if tile == SEAM else "sbuf"

    def walk_gather(eng, do_chunk, first, end):
        with eng.Fori(first, end) as i:
            for s in range(FIRST_RING):
                do_chunk(Chunk(0, FIRST_RING * i + s, s, i, FIRST_RING))

    def walk_first(eng, do):
        def body(i, n):
            for j in range(4):
                c = Chunk(1, n + 4 * i + j, j, n // 4 + i, RING)
                do(task(0, n + j, i, 0, 0, n + 4 * i + j, place_of(n + j), chunk=c))

        for n in range(4):
            do(task(0, n, 0, 0, 0, n, "dram", "top" if n == 0 else None,
                    chunk=Chunk(1, n, n, 0, RING)))
        with eng.Fori(0, SEAM // 4 - 1) as i:
            body(i, 4)
        body(0, SEAM)
        with eng.Fori(0, (CHUNKS - SEAM) // 4 - 1) as i:
            body(i, SEAM + 4)
        for n in range(CHUNKS, TILES):
            last = n == TILES - 1
            do(task(0, n, 0, 0, 0, n, "sbuf", "bottom" if last else None,
                    x_stage={CHUNKS: 0, CHUNKS + 2: 1, CHUNKS + 3: 2}.get(n),
                    y_stage=(0,) if last else (), then_last=n == TILES - 3))
        walk_head(do, 1, {0: (1,), 1: (2,)})

    def walk_head(do, b, y_stages={}):
        for k in range(HEAD):
            do(task(phase_q(b), 2 + k, 0, 0, b, k, "dram", "top" if k == 0 else None,
                    y_stage=y_stages.get(k, ()), then_last=k == 2))

    def walk_middle(eng, do, b, with_stats):
        q0 = phase_q(b)
        PAIRS = TILES - HEAD

        def body(i, p, x_stages=()):
            for j in range(4):
                pair = p + j // 2
                chunk = None
                if with_stats and j % 2 and 2 <= p < 2 + CHUNKS:
                    chunk = Chunk(b + 1, p - 2 + 2 * i + j // 2, j // 2,
                                  CHUNKS // RING + (CHUNKS // 2) * (b - 1) + p // 2 - 1 + i, 2)
                x_stage = dict(x_stages).get(j) if with_stats else None
                if j % 2 == 0:
                    tile = TILES - 1 - pair
                    do(task(q0, 6 + 2 * p + j, i, 1, b - 1, tile - 2 * i, place_of(tile),
                            "bottom" if pair == 0 else None, x_stage=x_stage, chunk=chunk))
                else:
                    tile, last = pair + HEAD, pair == PAIRS - 1
                    do(task(q0, 6 + 2 * p + j, i, 0, b, tile + 2 * i, place_of(tile),
                            "bottom" if last else None, x_stage=x_stage,
                            y_stage=(0,) if last else (), chunk=chunk,
                            then_last=pair == PAIRS - 2))

        def bodies(p, end):
            with eng.Fori(0, (end - p) // 2) as i:
                body(i, p)

        body(0, 0)
        bodies(2, CACHED - 2)
        body(0, CACHED - 2)
        bodies(CACHED, SEAM - HEAD)
        body(0, SEAM - HEAD)
        bodies(SEAM - HEAD + 2, PAIRS - 4)
        body(0, PAIRS - 4, ((0, 0), (2, 1)))
        body(0, PAIRS - 2, ((0, 2),))
        y_stages = {1: (1,), 3: (2,)} if with_stats else {0: (1,), 1: (2,)}
        for k in range(HEAD):
            do(task(q0, 6 + 2 * PAIRS + k, 0, 1, b - 1, HEAD - 1 - k, "dram",
                    "top" if k == HEAD - 1 else None, y_stage=y_stages.get(k, ()),
                    then_last=k == 2 and not with_stats))
        if with_stats:
            walk_head(do, b + 1)

    def walk_last(eng, do):
        q0 = phase_q(B)

        def body(i, k, n=4):
            for k in range(k, k + n):
                tile = TILES - 1 - k
                do(task(q0, 2 + k, i, 1, B - 1, tile - 4 * i, place_of(tile),
                        {TILES - 1: "bottom", 0: "top"}.get(tile)))

        body(0, 0, 2)
        with eng.Fori(0, (CACHED - 6) // 4) as i:
            body(i, 2)
        body(0, CACHED - 4)
        with eng.Fori(0, (SEAM - 4) // 4) as i:
            body(i, CACHED)
        body(0, TILES - 4)

    def walk(eng, do):
        walk_first(eng, do)
        with eng.Fori(1, B - 1) as b:
            walk_middle(eng, do, b, True)
        walk_middle(eng, do, B - 1, False)
        walk_last(eng, do)

    def number(k):
        return 4 * k.q + k.slot

    def after(k, back):
        if isinstance(k.q, int) and 4 * k.q + k.slot - back < 0:
            return None
        return 4 * k.q + (k.slot - back + 1)

    def y_image(k, stage):
        if k.layer == 1:
            return k.image + 1
        return k.image - (stage > 0)

    def helped(k):
        return (k.layer == 0 and isinstance(k.image, int) and k.image == 0
                and not (isinstance(k.tile, int) and k.tile >= TILES - 2))

    TASKS = 2 * B * TILES

    with ExitStack() as ctx:
        def sb(name, shape, dt):
            return ctx.enter_context(nc.sbuf_tensor(name, shape, dt))

        def sem(name):
            return ctx.enter_context(nc.semaphore(name))

        x_in = sb("x_in", [P, RING, W], F32)
        x_hat = sb("x_hat", [P, 2, W], F32)
        resid = sb("resid", [P, RING, W], F32)
        high = sb("high", [P, RING, W + 2], F16)
        low = sb("low", [P, RING, W + 2], F16)
        y_out = sb("y_out", [P, RING, W], F32)
        y_cache = sb("y_cache", [P, CACHED * W], F32)
        chunks = sb("chunks", [P, RING, W], F32)
        x_moments = sb("x_moments", [P, CHUNKS * 2 * 6], F32)
        y_moments = sb("y_moments", [P, (TILES - 1) * HALVES * 6], F32)
        y_moments_last = sb("y_moments_last", [P, HALVES * 6], F32)
        band = sb("band", [P, 2, TAPS, P], F32)
        band_abs = sb("band_abs", [P, 2, TAPS * P], F32)
        w_high = sb("w_high", [P, 2, TAPS, P], F16)
        w_low = sb("w_low", [P, 2, TAPS, P], F16)
        w_last = sb("w_last", [P, 2, TAPS, P], F16)
        w_max = sb("w_max", [P, 2], F32)
        w_max_all = sb("w_max_all", [P, 2], F32)
        w_pow2 = sb("w_pow2", [P, 2], F32)
        w_scale = sb("w_scale", [P, 2], F32)
        w_unscale = sb("w_unscale", [P, 2], F32)
        bias = sb("bias", [P, 2], F32)
        avg_x_sb = sb("avg_x_sb", [P, P], F32)
        avg_y_sb = sb("avg_y_sb", [P, P], F32)
        avg_y_last_sb = sb("avg_y_last_sb", [P, P], F32)
        edge_keep_sb = sb("edge_keep_sb", [P, 2], F32)
        mv = [sb(f"mv{l}", [P, 2], F32) for l in range(2)]
        mv_last = sb("mv_last", [P, 2], F32)
        diff = [sb(f"diff{l}", [P, 2], F32) for l in range(2)]
        var_eps = [sb(f"var_eps{l}", [P, 1], F32) for l in range(2)]
        guess = [sb(f"guess{l}", [P, 2], F32) for l in range(2)]
        tmp = [sb(f"tmp{l}", [P, 2], F32) for l in range(2)]
        fresh = [sb(f"fresh{l}", [P, 6], F32) for l in range(2)]
        affine = [sb(f"affine{l}", [P, 6], F32) for l in range(2)]

        conv = ctx.enter_context(nc.psum_tensor("conv", [P, 2, HALVES, BANK], F32))
        stat = [ctx.enter_context(nc.psum_tensor(f"stat{l}", [P, BANK], F32)) for l in range(2)]

        consts_loaded = sem("consts_loaded")
        band_zeroed = sem("band_zeroed")
        bands_loaded = sem("bands_loaded")
        max_found = sem("max_found")
        max_shared = sem("max_shared")
        scale_step = sem("scale_step")
        weights_ready = sem("weights_ready")
        stack_ready = sem("stack_ready")
        pads_zeroed = sem("pads_zeroed")
        loaded = [sem(f"loaded{s}") for s in range(RING)]
        edge_loaded = {(l, e): sem(f"edge_loaded_{l}_{e}") for l in range(2) for e in ("top", "bottom")}
        edge_dmas = {(0, "top"): 1, (0, "bottom"): 2 * STACK - 1, (1, "top"): 1,
                     (1, "bottom"): STACK - 1}
        first_loaded = [sem(f"first_loaded{s}") for s in range(FIRST_RING)]
        chunk_loaded = [sem(f"chunk_loaded{s}") for s in range(RING)]
        chunk_done = sem("chunk_done")
        x_hat_ready = sem("x_hat_ready")
        high_ready = sem("high_ready")
        low_ready = sem("low_ready")
        conv_done = sem("conv_done")
        y_ready = sem("y_ready")
        y_moments_done = sem("y_moments_done")
        stored = [sem(f"stored{s}") for s in range(RING)]
        chain = [sem("x_chain"), sem("y_chain")]
        mean_summed = [sem("x_mean_summed"), sem("y_mean_summed")]
        var_summed = [sem("x_var_summed"), sem("y_var_summed")]
        params_ready = [sem("x_params_ready"), sem("y_params_ready")]
        params_taken = [sem("x_params_taken"), sem("y_params_taken")]

        def split_low(eng, q, slot, last_tile=False):
            eng.wait_ge(high_ready, 4 * q + slot + 1)
            if last_tile:
                second = slice(LAST_K, 2 * LAST_K)
                eng.tensor_tensor(high[second, slot, 1:W + 1], x_hat[second, slot % 2, :],
                                  high[second, slot, 1:W + 1], ALU.subtract).then_inc(low_ready, 1)
            else:
                eng.tensor_tensor(low[:, slot, 1:W + 1], x_hat[:, slot % 2, :],
                                  high[:, slot, 1:W + 1], ALU.subtract).then_inc(low_ready, 1)

        def chunk_place(c):
            if c.ring == FIRST_RING:
                return y_cache[:, c.slot * W:(c.slot + 1) * W], first_loaded[c.slot]
            return chunks[:, c.slot, :], chunk_loaded[c.slot]

        def in_cache(tile, first, end):
            return y_cache[first:end, bass.ds((tile - SEAM) * W, W)]

        block = ctx.enter_context(nc.Block())

        @block.sync
        def _(sp):
            place_register = sp.alloc_register("place")
            wait_registers = [sp.alloc_register(f"wait_count{n}") for n in range(3)]

            def load_chunk(c):
                src = x[c.image, :, bass.ds(c.index * ROWS_IN, ROWS_IN), :].rearrange("c r w -> r c w")
                if not (isinstance(c.use, int) and c.use == 0):
                    sp.wait_ge(chunk_done, CHUNKS * c.image + c.index - c.ring + 1)
                buffer, signal = chunk_place(c)
                sp.dma_start(buffer, src).then_inc(signal, 16)

            for s in range(FIRST_RING):
                load_chunk(Chunk(0, s, s, 0, FIRST_RING))
            walk_gather(sp, load_chunk, 1, CHUNKS // FIRST_RING)

            def held(value, least, most):
                if isinstance(value, int):
                    return value
                sp.reg_mov(place_register, value)
                return sp.snap(place_register, min_val=least, max_val=most)

            def load_tile(k):
                if k.layer == 1 and k.cached:
                    offset = held((k.tile - SEAM) * W, W, (CACHED - 1) * W)
                elif k.edge is None:
                    first_row = held(k.tile * ROWS_OUT - 1, 0, H - ROWS_IN)
                if k.layer == 1 and k.edge == "bottom":
                    q0 = phase_q(k.image + 1)
                    final = isinstance(k.image, int) and k.image == B - 1
                    counts = (16 * (q0 + (0 if final else 1)), 16 * (q0 - (1 if final else 0)),
                              TILES * (k.image + 1))
                    for register, count in zip(wait_registers, counts):
                        sp.reg_mov(register, count)
                    for s in range(RING):
                        sp.wait_ge(stored[s], wait_registers[s // 2])
                    sp.wait_ge(y_moments_done, wait_registers[2])
                elif (done := after(k, RING)) is not None:
                    sp.wait_ge(high_ready, done)

                def rows(first, n):
                    if k.layer == 0:
                        return x[k.image, :, bass.ds(first, n), :].rearrange("c r w -> r c w")
                    return y[k.image, bass.ds(first, n), :, :].rearrange("r c w -> (r c) w")

                if k.layer == 1 and k.cached:
                    above = (rows(SEAM * ROWS_OUT - 1, 1) if k.seam
                             else y_cache[P - 2 * C:P - C, bass.ds(offset - W, W)])
                    sp.dma_start(y_cache[0:C, bass.ds(offset, W)], above
                                 ).then_inc(loaded[k.slot], 16)
                    if k.edge == "bottom":
                        for n in range(1, STACK):
                            sp.dma_start(y_cache[n * LAST_K:n * LAST_K + C, bass.ds(offset, W)], above
                                         ).then_inc(edge_loaded[1, "bottom"], 16)
                elif k.edge == "top":
                    sp.dma_start(x_in[0:C, k.slot, :], rows(1, 1)
                                 ).then_inc(edge_loaded[k.layer, "top"], 16)
                    sp.dma_start(x_in[C:P, k.slot, :], rows(0, ROWS_IN - 1)
                                 ).then_inc(loaded[k.slot], 16)
                elif k.edge == "bottom":
                    n = LAST_ROWS + 1
                    for p in range(0, STACK * LAST_K, LAST_K):
                        signal = edge_loaded[0, "bottom"] if p else loaded[k.slot]
                        sp.dma_start(x_in[p:p + n * C, k.slot, :], rows(H - n, n)
                                     ).then_inc(signal, 16)
                        sp.dma_start(x_in[p + n * C:p + LAST_K, k.slot, :], rows(H - 1, 1)
                                     ).then_inc(edge_loaded[0, "bottom"], 16)
                else:
                    sp.dma_start(x_in[:, k.slot, :], rows(first_row, ROWS_IN)
                                 ).then_inc(loaded[k.slot], 16)

                if k.chunk is not None:
                    load_chunk(k.chunk)

            walk(sp, load_tile)

        @block.scalar
        def _(act):
            act.wait_ge(band_zeroed, 1)
            for l, weight in enumerate((weight0, weight1)):
                for r in range(1, ROWS_OUT + 1):
                    act.dma_start(band[(r - 1) * C:(r + 2) * C, l, :, r * C:(r + 1) * C],
                                  weight.rearrange("kh ci kw co -> (kh ci) kw co")
                                  ).then_inc(bands_loaded, 16)
            with nc.allow_non_contiguous_dma(reason="eight values of bias"):
                for l, b in enumerate((bias0, bias1)):
                    for r in range(ROWS_IN):
                        act.dma_start(bias[r * C:(r + 1) * C, l:l + 1], b).then_inc(consts_loaded, 16)
                act.dma_start(edge_keep_sb[:, :], edge_keep).then_inc(consts_loaded, 16)
            for dst, src in ((avg_x_sb, avg_x), (avg_y_sb, avg_y),
                             (avg_y_last_sb, avg_y_last)):
                act.dma_start(dst[:, :], src).then_inc(consts_loaded, 16)
            act.wait_ge(consts_loaded, 16 * (2 * ROWS_IN + 4))
            act.wait_ge(pads_zeroed, 2)
            act.wait_ge(weights_ready, 1)
            for n, w in enumerate((w_high, w_high, w_low)):
                rows_n = slice(n * LAST_K, (n + 1) * LAST_K)
                for first in range(0, P, LAST_K):
                    last = act.copy(w_last[rows_n, :, :, first:first + LAST_K], w[rows_n, :, :, rows_n])
            last.then_inc(stack_ready, 1)

            def prepare(k):
                l = k.layer
                src = in_cache(k.tile, 0, P) if l == 1 and k.cached else x_in[:, k.slot, :]

                def add_bias():
                    nc.scalar.activation(resid[:, k.slot, :], src, ACT.Identity,
                                         scale=1.0, bias=bias[:, l:l + 1])

                act.wait_ge(loaded[k.slot], 16 * (k.q + 1))
                if k.edge:
                    act.wait_ge(edge_loaded[l, k.edge], 16 * edge_dmas[l, k.edge] * (k.image + 1))
                if (done := after(k, RING)) is not None:
                    act.wait_ge(y_ready, done)
                first = k.edge == ("top", "bottom")[l]
                if first:
                    add_bias()
                    act.wait_ge(params_ready[l], k.image + 1)
                    act.copy(affine[l][:, :], fresh[l][:, :]).then_inc(params_taken[l], 1)
                    act.wait_ge(params_taken[l], k.image + 1)
                if (done := after(k, 2)) is not None:
                    act.wait_ge(low_ready, done)
                a = {None: 0, "top": 2, "bottom": 4}[k.edge]
                nc.scalar.activation(x_hat[:, k.slot % 2, :], src, ACT.Identity,
                                     scale=affine[l][:, a:a + 1], bias=affine[l][:, a + 1:a + 2]
                                     ).then_inc(x_hat_ready, 1)
                if not first:
                    add_bias()
                act.wait_ge(x_hat_ready, number(k) + 1)
                act.copy(high[:, k.slot, 1:W + 1], x_hat[:, k.slot % 2, :]).then_inc(high_ready, 1)

            walk(act, prepare)

        @block.tensor
        def _(pe):
            def sum_mean(l, image):
                pe.wait_ge(chain[l], image * (KX, KY)[l] + 1 + l)
                if l == 0:
                    pe.matmul(stat[0][:, 0:1], avg_x_sb[:, :], mv[0][:, 0:1], start=True,
                              stop=True).then_inc(mean_summed[0], 1)
                else:
                    pe.matmul(stat[1][:, 0:1], avg_y_sb[:, :], mv[1][:, 0:1], start=True, stop=False)
                    pe.matmul(stat[1][:, 0:1], avg_y_last_sb[:, :], mv_last[:, 0:1], start=False,
                              stop=True).then_inc(mean_summed[1], 1)

            def sum_var(l, image):
                pe.wait_ge(chain[l], image * (KX, KY)[l] + 3 + 3 * l)
                if l == 0:
                    pe.matmul(stat[0][:, 2:4], avg_x_sb[:, :], mv[0][:, :], start=True,
                              stop=True).then_inc(var_summed[0], 1)
                else:
                    pe.matmul(stat[1][:, 2:4], avg_y_sb[:, :], mv[1][:, :], start=True, stop=False)
                    pe.matmul(stat[1][:, 2:4], avg_y_last_sb[:, :], mv_last[:, :], start=False,
                              stop=True).then_inc(var_summed[1], 1)

            def convolve(k):
                l, ps = k.layer, k.slot % 2
                pe.wait_ge(high_ready, number(k) + 1)
                if (done := after(k, 2)) is not None:
                    pe.wait_ge(y_ready, done)
                if k.edge == "bottom":
                    products = ((w_last, high, STACK * LAST_K),)
                    pe.wait_ge(low_ready, number(k) + 1)
                else:
                    products = ((w_high, high, P), (w_low, high, P), (w_high, low, P))
                for part, (w, v, kk) in enumerate(products):
                    if part == 2:
                        pe.wait_ge(low_ready, number(k) + 1)
                    for kw in range(TAPS):
                        for half in range(HALVES):
                            last = pe.matmul(
                                conv[:, ps, half, :], w[0:kk, l, kw, :],
                                v[0:kk, k.slot, half * BANK + kw:half * BANK + kw + BANK],
                                start=(part == 0 and kw == 0),
                                stop=(part == len(products) - 1 and kw == TAPS - 1))
                last.then_inc(conv_done, 1)
                if k.x_stage == 1:
                    sum_mean(0, k.image + 1 if l == 0 else k.image + 2)
                if k.x_stage == 2:
                    sum_var(0, k.image + 1 if l == 0 else k.image + 2)
                for stage in k.y_stage:
                    if stage == 1:
                        sum_mean(1, y_image(k, stage))
                    if stage == 2:
                        sum_var(1, y_image(k, stage))

            pe.wait_ge(consts_loaded, 16 * (2 * ROWS_IN + 4))
            sum_mean(0, 0)
            sum_var(0, 0)
            pe.wait_ge(stack_ready, 1)
            walk(pe, convolve)

        @block.vector
        def _(dve):
            nc.vector.memset(high[:, :, :], 0.0).then_inc(pads_zeroed, 1)
            nc.vector.memset(low[:, :, :], 0.0).then_inc(pads_zeroed, 1)
            nc.vector.memset(mv_last[:, :], 0.0).then_inc(scale_step, 1)
            steps = [1]

            def step(ins):
                steps[0] += 1
                ins.then_inc(scale_step, 1)
                dve.wait_ge(scale_step, steps[0])

            def scale_weights():
                dve.wait_ge(bands_loaded, 2 * ROWS_OUT * 16)
                step(nc.vector.tensor_scalar(
                    band_abs[:, :, :].bitcast(I32),
                    band[:, :, :, :].rearrange("p l k n -> p l (k n)").bitcast(I32),
                    0x7FFFFFFF, None, ALU.bitwise_and))
                for l in range(2):
                    nc.vector.reduce_max(w_max[:, l:l + 1], band_abs[:, l, :], AX_X
                                         ).then_inc(max_found, 1)
                dve.wait_ge(max_shared, 1)
                step(nc.vector.tensor_scalar(w_max[:, :], w_max_all[:, :], 2.0 ** -100, None, ALU.max))
                step(nc.vector.tensor_scalar(w_pow2[:, :].bitcast(I32), w_max[:, :].bitcast(I32),
                                             0x7F800000, None, ALU.bitwise_and))
                step(nc.vector.tensor_scalar(w_unscale[:, :], w_pow2[:, :], 1.0 / WEIGHT_TOP, None,
                                             ALU.mult))
                step(nc.vector.reciprocal(w_scale[:, :], w_unscale[:, :]))
                for l in range(2):
                    step(nc.vector.tensor_scalar(w_high[:, l, :, :], band[:, l, :, :],
                                                 w_scale[:, l:l + 1], None, ALU.mult))
                    last = nc.vector.scalar_tensor_tensor(
                        w_low[:, l, :, :], band[:, l, :, :], w_scale[:, l:l + 1], w_high[:, l, :, :],
                        ALU.mult, ALU.subtract)
                    if l == 0:
                        step(last)
                last.then_inc(weights_ready, 1)

            def gather(c):
                buffer, signal = chunk_place(c)
                dve.wait_ge(signal, 16 * (c.use + 1))
                nc.vector.bn_stats(x_moments[:, bass.ds(c.index * 12, 6)], buffer[:, 0:BANK])
                nc.vector.bn_stats(x_moments[:, bass.ds(c.index * 12 + 6, 6)],
                                   buffer[:, BANK:2 * BANK]).then_inc(chunk_done, 1)

            def linker(l, image, start):
                at = [start]

                def link(ins):
                    at[0] += 1
                    ins.then_inc(chain[l], 1)
                    dve.wait_ge(chain[l], image * (KX, KY)[l] + at[0])
                return link

            def aggregate(l, image):
                link = linker(l, image, 0)
                if l == 0:
                    dve.wait_ge(chunk_done, CHUNKS * (image + 1))
                    nc.vector.memset(tmp[0][:, :], 0.0)
                    link(nc.vector.bn_aggr(mv[0][:, :], x_moments[:, :]))
                else:
                    dve.wait_ge(y_moments_done, TILES * (image + 1))
                    nc.vector.memset(tmp[1][:, :], 0.0)
                    nc.vector.bn_aggr(mv[1][:, :], y_moments[:, :]).then_inc(chain[1], 1)
                    nc.vector.bn_aggr(mv_last[0:LAST_K, :], y_moments_last[0:LAST_K, :]
                                      ).then_inc(chain[1], 1)
                    dve.wait_ge(chain[1], image * KY + 2)

            def distance(l, image):
                link = linker(l, image, 1 + l)
                dve.wait_ge(mean_summed[l], image + 1)
                for m, p in ((mv[l], P),) + (((mv_last, LAST_K),) if l else ()):
                    d = diff[l][0:p, 0:1] if p == P else diff[l][0:p, 1:2]
                    link(nc.vector.tensor_tensor(d, m[0:p, 0:1], stat[l][0:p, 0:1], ALU.subtract))
                    link(nc.vector.scalar_tensor_tensor(m[0:p, 1:2], d, d, m[0:p, 1:2],
                                                        ALU.mult, ALU.add))

            def finish(l, image):
                link = linker(l, image, 3 + 3 * l)
                dve.wait_ge(var_summed[l], image + 1)
                link(nc.vector.tensor_scalar(var_eps[l][:, :], stat[l][:, 3:4], EPS, None, ALU.add))
                g = guess[l]
                link(nc.vector.tensor_scalar(g[:, 0:1].bitcast(I32), var_eps[l][:, :].bitcast(I32),
                                             -0.5, float(0x5F3759DF), ALU.mult, ALU.add))
                for n in range(3):
                    a, b = g[:, n % 2:n % 2 + 1], g[:, 1 - n % 2:2 - n % 2]
                    link(nc.vector.scalar_tensor_tensor(tmp[l][:, 0:1], a, var_eps[l][:, 0:1], a,
                                                        ALU.mult, ALU.mult))
                    link(nc.vector.tensor_scalar(tmp[l][:, 1:2], tmp[l][:, 0:1], -0.5, 1.5,
                                                 ALU.mult, ALU.add))
                    if n < 2:
                        link(nc.vector.tensor_tensor(b, a, tmp[l][:, 1:2], ALU.mult))
                if not (isinstance(image, int) and image == 0):
                    dve.wait_ge(params_taken[l], image)
                link(nc.vector.tensor_tensor(fresh[l][:, 0:1], a, tmp[l][:, 1:2], ALU.mult))
                link(nc.vector.scalar_tensor_tensor(fresh[l][:, 1:2], stat[l][:, 2:3], -1.0,
                                                    fresh[l][:, 0:1], ALU.mult, ALU.mult))
                nc.vector.tensor_scalar(fresh[l][:, 2:4], fresh[l][:, 0:2], edge_keep_sb[:, 0:1],
                                        None, ALU.mult)
                nc.vector.tensor_scalar(fresh[l][:, 4:6], fresh[l][:, 0:2], edge_keep_sb[:, 1:2],
                                        None, ALU.mult).then_inc(params_ready[l], 1)

            def evacuate(k):
                l = k.layer
                dve.wait_ge(conv_done, number(k) + 1)
                if l == 0 and k.cached:
                    dst = in_cache(k.tile, 0, P)
                else:
                    dst = y_out[:, k.slot, :]
                    if not (isinstance(k.q, int) and k.q == 0):
                        dve.wait_ge(stored[k.slot], 16 * k.q)
                nc.vector.scalar_tensor_tensor(
                    dst, conv[:, k.slot % 2, :, :].rearrange("p h n -> p (h n)"),
                    w_unscale[:, l:l + 1], resid[:, k.slot, :], ALU.mult, ALU.add
                    ).then_inc(y_ready, 1)
                last_two = isinstance(k.q, int) and number(k) >= TASKS - 2
                if isinstance(k.q, int) and number(k) == TILES - 2:
                    dve.wait_ge(low_ready, TILES)
                if not helped(k) and not last_two:
                    split_low(nc.vector, k.q + (k.slot + 2) // RING, (k.slot + 2) % RING,
                              k.then_last)
                if l == 0:
                    dve.wait_ge(y_ready, number(k) + 1)
                    for half in range(HALVES):
                        rows = LAST_K if k.edge == "bottom" else P
                        if k.cached:
                            src = y_cache[0:rows, bass.ds((k.tile - SEAM) * W + half * BANK, BANK)]
                        else:
                            src = y_out[:, k.slot, half * BANK:(half + 1) * BANK]
                        if k.edge == "bottom":
                            last = nc.vector.bn_stats(y_moments_last[0:LAST_K, half * 6:half * 6 + 6],
                                                      src)
                        else:
                            last = nc.vector.bn_stats(
                                y_moments[:, bass.ds((k.tile * HALVES + half) * 6, 6)], src)
                    last.then_inc(y_moments_done, 1)
                if k.chunk is not None:
                    gather(k.chunk)
                if k.x_stage is not None:
                    (aggregate, distance, finish)[k.x_stage](0, k.image + 1 if l == 0 else k.image + 2)
                for stage in k.y_stage:
                    (aggregate, distance, finish)[stage](1, y_image(k, stage))

            walk_gather(dve, gather, 0, CHUNKS // FIRST_RING // 2)
            scale_weights()
            walk_gather(dve, gather, CHUNKS // FIRST_RING // 2, CHUNKS // FIRST_RING)
            dve.wait_ge(consts_loaded, 16 * (2 * ROWS_IN + 4))
            aggregate(0, 0)
            distance(0, 0)
            finish(0, 0)
            walk(dve, evacuate)

        @block.gpsimd
        def _(pool):
            nc.gpsimd.memset(band[:, :, :, :], 0.0).then_inc(band_zeroed, 1)
            pool.wait_ge(max_found, 2)
            nc.gpsimd.partition_all_reduce(w_max_all[:, :], w_max[:, :], P,
                                           bass.bass_isa.ReduceOp.max).then_inc(max_shared, 1)

            tile_register = pool.alloc_register("tile")

            def store(k):
                if helped(k):
                    if (done := after(k, 2)) is not None:
                        pool.wait_ge(conv_done, done)
                    if k.then_last:
                        pool.wait_ge(low_ready, number(k) + 2)
                    split_low(nc.gpsimd, k.q + (k.slot + 2) // RING, (k.slot + 2) % RING,
                              k.then_last)
                stays = k.layer == 0 and k.cached
                tile = k.tile
                if not isinstance(tile, int) or (stays and not isinstance(k.q, int)):
                    pool.reg_mov(tile_register, tile)
                    tile = pool.snap(tile_register, min_val=SEAM + (not k.seam) if stays else 0,
                                     max_val=TILES - 1 if k.edge == "bottom" else TILES - 2)
                if stays:
                    pool.wait_ge(y_moments_done, TILES * k.image + k.tile)
                    pool.wait_ge(y_ready, number(k) + 1)
                    dst = (y[k.image, SEAM * ROWS_OUT, :, :] if k.seam
                           else in_cache(tile - 1, P - C, P))
                    pool.dma_start(dst, in_cache(tile, C, 2 * C)).then_inc(stored[k.slot], 16)
                    return
                pool.wait_ge(y_ready, number(k) + 1)
                n = LAST_ROWS if k.edge == "bottom" else ROWS_OUT
                if k.layer == 0:
                    dst = y[k.image, bass.ds(tile * ROWS_OUT, n), :, :].rearrange("r c w -> (r c) w")
                else:
                    dst = out[k.image, :, bass.ds(tile * ROWS_OUT, n), :].rearrange("c r w -> r c w")
                pool.dma_start(dst, y_out[C:C + n * C, k.slot, :]).then_inc(stored[k.slot], 16)

            pool.wait_ge(pads_zeroed, 2)
            split_low(nc.gpsimd, 0, 0)
            split_low(nc.gpsimd, 0, 1)
            walk(pool, store)
            for s in range(RING):
                pool.wait_ge(stored[s], 16 * (TASKS // RING))


def constants(H, W):
    import numpy as np

    tiles = -(-H // ROWS_OUT)
    last_rows = H - (tiles - 1) * ROWS_OUT
    group_size = C // GROUPS * H * W
    p = np.arange(P)
    row, group = p // C, p % C // (C // GROUPS)
    inside = (row >= 1) & (row <= ROWS_OUT)
    inside_last = (row >= 1) & (row <= last_rows)
    same = group[:, None] == group[None, :]
    row_last = row % (LAST_K // C)
    return {
        "avg_x": same * (GROUPS / P),
        "avg_y": same * inside[:, None] * ((tiles - 1) * W / group_size),
        "avg_y_last": same * inside_last[:, None] * (W / group_size),
        "edge_keep": np.stack([row >= 1, row_last <= last_rows], 1),
    }


def kernel(**inputs):
    import numpy as np
    import concourse.bacc as bacc
    from concourse.bass_utils import run_bass_kernel_spmd

    x = np.ascontiguousarray(inputs["x"])
    arrays = {"x": x}
    for l in range(2):
        arrays[f"weight{l}"] = np.ascontiguousarray(
            np.transpose(np.asarray(inputs[f"L{l}_conv_weight"]), (2, 1, 3, 0)))
        arrays[f"bias{l}"] = np.ascontiguousarray(np.asarray(inputs[f"L{l}_conv_bias"]).reshape(C, 1))
    for name, a in constants(x.shape[2], x.shape[3]).items():
        arrays[name] = np.ascontiguousarray(a.astype(np.float32))

    nc = bacc.Bacc("TRN2", target_bir_lowering=False, num_devices=1)
    aps = {n: nc.dram_tensor(n, a.shape, mybir.dt.from_np(a.dtype), kind="ExternalInput").ap()
           for n, a in arrays.items()}
    out = nc.dram_tensor("out", x.shape, F32, kind="ExternalOutput").ap()
    conv_preact_program(nc, out=out, **aps)
    r = run_bass_kernel_spmd(nc, [arrays], core_ids=[0])
    return r.results[0]["out"]
```
